# Optimizing a Trainium2 kernel written in Bass

```python
import numpy as np
import jax
import jax.numpy as jnp

def _softmax(x, axis=-1):
    return jax.nn.softmax(x, axis=axis)

def _gelu(x):
    return jax.nn.gelu(x, approximate=True)

def _silu(x):
    return jax.nn.silu(x)

def _sigmoid(x):
    return jax.nn.sigmoid(x)

def _layernorm(x, axis=-1, eps=1e-05):
    m = jnp.mean(x, axis=axis, keepdims=True)
    v = jnp.var(x, axis=axis, keepdims=True)
    return (x - m) / jnp.sqrt(v + eps)

def _scatter_add(tgt, idx, src, axis=0):
    return tgt.at[idx].add(src)

def _segment_sum(src, seg, n):
    return jax.ops.segment_sum(src, seg, n)
kernel_name = 'mk_adaln_d2_jaxref_r8_25bd88'

def setup_inputs(seed: int=0):
    np.random.seed(seed)
    _w = jnp.asarray

    def _L0_attn_setup():
        import jax, jax.numpy as jnp
        import numpy as np
        DIM = 128
        H = 16
        DH = DIM // H
        K = 4
        B = 8
        N = 256
        EPS = 1e-06

        def _depthwise_conv_silu(x, w, n):
            pad = K // 2
            y = jax.lax.conv_general_dilated(x.transpose(0, 2, 1), w, window_strides=(1,), padding=[(pad, pad)], dimension_numbers=('NCH', 'OIH', 'NCH'), feature_group_count=x.shape[-1])
            y = y[..., :n]
            return jax.nn.silu(y).transpose(0, 2, 1)

        def _l2norm(x):
            return x / (jnp.linalg.norm(x, axis=-1, keepdims=True) + EPS)

        def _forward(x, Wq, bq, Wk, bk, Wv, bv, Wa, ba, Wb, bb, conv_q, conv_k, conv_v, Wo, bo):
            b_, n_, c_ = x.shape
            q = _l2norm(_depthwise_conv_silu(jax.nn.silu(x @ Wq.T + bq), conv_q, n_))
            k = _l2norm(_depthwise_conv_silu(jax.nn.silu(x @ Wk.T + bk), conv_k, n_))
            v = _depthwise_conv_silu(jax.nn.silu(x @ Wv.T + bv), conv_v, n_)
            a = jax.nn.sigmoid(x @ Wa.T + ba)
            bgate = jax.nn.sigmoid(x @ Wb.T + bb)
            q = q.reshape(b_, n_, H, DH).transpose(1, 0, 2, 3)
            k = k.reshape(b_, n_, H, DH).transpose(1, 0, 2, 3)
            v = v.reshape(b_, n_, H, DH).transpose(1, 0, 2, 3)
            a = a.transpose(1, 0, 2)
            bgate = bgate.transpose(1, 0, 2)
            S0 = jnp.zeros((b_, H, DH, DH), x.dtype)

            def step(S, inp):
                qt, kt, vt, at, bt = inp
                at = at[..., None, None]
                bt = bt[..., None, None]
                Sk = jnp.einsum('bhde,bhe->bhd', S, kt)
                outer_Sk_k = Sk[..., :, None] * kt[..., None, :]
                outer_v_k = vt[..., :, None] * kt[..., None, :]
                S_new = at * S - at * bt * outer_Sk_k + bt * outer_v_k
                ot = jnp.einsum('bhd,bhde->bhe', qt, S_new)
                return (S_new, ot)
            _, O = jax.lax.scan(step, S0, (q, k, v, a, bgate))
            O = O.transpose(1, 0, 2, 3).reshape(b_, n_, c_)
            return O @ Wo.T + bo
        key = jax.random.key(seed)
        ks = jax.random.split(key, 16)
        s = 1.0 / np.sqrt(DIM)
        d = dict(x=jax.random.normal(ks[0], (B, N, DIM), jnp.float32), Wq=jax.random.normal(ks[1], (DIM, DIM), jnp.float32) * s, bq=jnp.zeros((DIM,), jnp.float32), Wk=jax.random.normal(ks[2], (DIM, DIM), jnp.float32) * s, bk=jnp.zeros((DIM,), jnp.float32), Wv=jax.random.normal(ks[3], (DIM, DIM), jnp.float32) * s, bv=jnp.zeros((DIM,), jnp.float32), Wa=jax.random.normal(ks[4], (H, DIM), jnp.float32) * s, ba=jnp.zeros((H,), jnp.float32), Wb=jax.random.normal(ks[5], (H, DIM), jnp.float32) * s, bb=jnp.zeros((H,), jnp.float32), conv_q=jax.random.normal(ks[6], (DIM, 1, K), jnp.float32) * 0.5, conv_k=jax.random.normal(ks[7], (DIM, 1, K), jnp.float32) * 0.5, conv_v=jax.random.normal(ks[8], (DIM, 1, K), jnp.float32) * 0.5, Wo=jax.random.normal(ks[9], (DIM, DIM), jnp.float32) * s, bo=jnp.zeros((DIM,), jnp.float32))
        return d
    _L0_attn_in = _L0_attn_setup()

    def _L0_ffn_setup():
        import jax, jax.numpy as jnp
        import numpy as np
        B, T, D, E, H, K = (2, 256, 128, 8, 512, 2)
        key = jax.random.key(seed)
        ks = jax.random.split(key, 8)
        s = 0.02
        return {'x': jax.random.normal(ks[0], (B, T, D), jnp.float32), 'rw1': jax.random.normal(ks[1], (D, D), jnp.float32) * s, 'rb1': jnp.zeros((D,), jnp.float32), 'rw2': jax.random.normal(ks[2], (D, E), jnp.float32) * s, 'rb2': jnp.zeros((E,), jnp.float32), 'we1': jax.random.normal(ks[3], (E, D, H), jnp.float32) * s, 'be1': jnp.zeros((E, H), jnp.float32), 'we2': jax.random.normal(ks[4], (E, H, D), jnp.float32) * s, 'be2': jnp.zeros((E, D), jnp.float32)}
    _L0_ffn_in = _L0_ffn_setup()
    _L0_c = _w((lambda *s: np.random.randn(*s).astype(np.float32) * 0.05)(8, 128))
    _L0_wmod = _w((lambda *s: np.random.randn(*s).astype(np.float32) * 0.05)(128, 6 * 128) * 128 ** (-0.5))

    def _L1_attn_setup():
        import jax, jax.numpy as jnp
        import numpy as np
        from jax import lax
        B, S, D_MODEL, H, D_CONV, CHUNK = (8, 512, 128, 16, 4, 64)
        D_INNER = D_MODEL

        def _segsum(a):
            T = a.shape[-1]
            lower_strict = jnp.tril(jnp.ones((T, T), bool), -1)
            lower = jnp.tril(jnp.ones((T, T), bool), 0)
            xr = jnp.where(lower_strict, a[..., :, None], 0.0)
            s = jnp.cumsum(xr, axis=-2)
            return jnp.where(lower, s, -jnp.inf)

        def _ssd(x, A, l):
            b, s, h, n = x.shape
            c = s // l
            x = x.reshape(b, c, l, h, n)
            A = A.reshape(b, c, l, h).transpose(0, 3, 1, 2)
            A_cumsum = jnp.cumsum(A, axis=-1)
            L_log = _segsum(A)
            L = jnp.exp(L_log - jnp.max(L_log, axis=-1, keepdims=True))
            norm_diag = L.sum(-1).transpose(0, 2, 3, 1)
            Y_diag = jnp.einsum('bhcls,bcshn->bclhn', L, x)
            decay_states = A_cumsum[..., -1:] - A_cumsum
            decay_states = jnp.exp(decay_states - jnp.max(decay_states, axis=-1, keepdims=True))
            norm_decay = decay_states.sum(-1).transpose(0, 2, 1)
            states = jnp.einsum('bhcl,bclhn->bchn', decay_states, x)
            norm_decay = jnp.pad(norm_decay, ((0, 0), (1, 0), (0, 0)))
            states = jnp.pad(states, ((0, 0), (1, 0), (0, 0), (0, 0)))
            decay_chunk = _segsum(jnp.pad(A_cumsum[..., -1], ((0, 0), (0, 0), (1, 0))))
            decay_chunk = jnp.exp(decay_chunk - jnp.max(decay_chunk, axis=-1, keepdims=True))
            norm_decay = jnp.einsum('bhzc,bch->bzh', decay_chunk, norm_decay)[:, :-1]
            states = jnp.einsum('bhzc,bchn->bzhn', decay_chunk, states)[:, :-1]
            state_decay_out = jnp.exp(A_cumsum - jnp.max(A_cumsum, axis=-1, keepdims=True))
            norm_off = jnp.einsum('bch,bhcl->bclh', norm_decay, state_decay_out)
            Y_off = jnp.einsum('bchn,bhcl->bclhn', states, state_decay_out)
            Y = (Y_diag + Y_off).reshape(b, s, h, n)
            norm = (norm_diag + norm_off).reshape(b, s, h)
            return Y / norm[..., None]
        key = jax.random.key(seed)
        ks = jax.random.split(key, 6)
        x = jax.random.normal(ks[0], (B, S, D_MODEL), jnp.float32)
        in_proj_w = jax.random.normal(ks[1], (D_INNER + H, D_MODEL), jnp.float32) * 0.02
        conv_w = jax.random.normal(ks[2], (D_INNER, 1, D_CONV), jnp.float32) * 0.3
        conv_b = jnp.zeros((D_INNER,), jnp.float32)
        w_base = jax.random.uniform(ks[3], (H,), jnp.float32, minval=-0.5, maxval=0.5)
        out_proj_w = jax.random.normal(ks[4], (D_MODEL, D_INNER), jnp.float32) * 0.02
        return {'x': x, 'in_proj_w': in_proj_w, 'conv_w': conv_w, 'conv_b': conv_b, 'w_base': w_base, 'out_proj_w': out_proj_w}
    _L1_attn_in = _L1_attn_setup()

    def _L1_ffn_setup():
        import jax, jax.numpy as jnp
        import numpy as np
        D_MODEL = 128
        EXPANSION = 4
        D_HIDDEN = D_MODEL * EXPANSION
        NUM_STAGES = int(np.log2(D_HIDDEN))

        def butterfly(y, weights, dim):
            lead = y.shape[:-1]
            for stage in range(weights.shape[0]):
                s = 2 ** stage
                nb = dim // (2 * s)
                yr = y.reshape(*lead, nb, 2, s)
                a = yr[..., 0, :]
                b = yr[..., 1, :]
                w = weights[stage].reshape(nb, s, 2, 2)
                na = w[..., 0, 0] * a + w[..., 0, 1] * b
                nb2 = w[..., 1, 0] * a + w[..., 1, 1] * b
                y = jnp.stack([na, nb2], axis=-2).reshape(*lead, dim)
            return y
        key = jax.random.key(seed)
        ks = jax.random.split(key, 6)
        B, S = (4, 256)
        x = jax.random.normal(ks[0], (B, S, D_MODEL), jnp.float32)
        W_exp = jax.random.normal(ks[1], (D_MODEL, D_HIDDEN), jnp.float32) * 0.02
        b_exp = jnp.zeros((D_HIDDEN,), jnp.float32)
        up_weights = jax.random.normal(ks[2], (NUM_STAGES, D_HIDDEN // 2, 2, 2), jnp.float32) * 0.02
        up_bias = jnp.zeros((D_HIDDEN,), jnp.float32)
        down_weights = jax.random.normal(ks[3], (NUM_STAGES, D_HIDDEN // 2, 2, 2), jnp.float32) * 0.02
        W_con = jax.random.normal(ks[4], (D_HIDDEN, D_MODEL), jnp.float32) * 0.02
        b_con = jnp.zeros((D_MODEL,), jnp.float32)
        down_bias = jnp.zeros((D_MODEL,), jnp.float32)
        return dict(x=x, W_exp=W_exp, b_exp=b_exp, up_weights=up_weights, up_bias=up_bias, down_weights=down_weights, W_con=W_con, b_con=b_con, down_bias=down_bias)
    _L1_ffn_in = _L1_ffn_setup()
    _L1_c = _w((lambda *s: np.random.randn(*s).astype(np.float32) * 0.05)(8, 128))
    _L1_wmod = _w((lambda *s: np.random.randn(*s).astype(np.float32) * 0.05)(128, 6 * 128) * 128 ** (-0.5))
    _d = {'L0_attn_x': _L0_attn_in['x'], 'L0_attn_Wq': _L0_attn_in['Wq'], 'L0_attn_bq': _L0_attn_in['bq'], 'L0_attn_Wk': _L0_attn_in['Wk'], 'L0_attn_bk': _L0_attn_in['bk'], 'L0_attn_Wv': _L0_attn_in['Wv'], 'L0_attn_bv': _L0_attn_in['bv'], 'L0_attn_Wa': _L0_attn_in['Wa'], 'L0_attn_ba': _L0_attn_in['ba'], 'L0_attn_Wb': _L0_attn_in['Wb'], 'L0_attn_bb': _L0_attn_in['bb'], 'L0_attn_conv_q': _L0_attn_in['conv_q'], 'L0_attn_conv_k': _L0_attn_in['conv_k'], 'L0_attn_conv_v': _L0_attn_in['conv_v'], 'L0_attn_Wo': _L0_attn_in['Wo'], 'L0_attn_bo': _L0_attn_in['bo'], 'L0_ffn_rw1': _L0_ffn_in['rw1'], 'L0_ffn_rb1': _L0_ffn_in['rb1'], 'L0_ffn_rw2': _L0_ffn_in['rw2'], 'L0_ffn_rb2': _L0_ffn_in['rb2'], 'L0_ffn_we1': _L0_ffn_in['we1'], 'L0_ffn_be1': _L0_ffn_in['be1'], 'L0_ffn_we2': _L0_ffn_in['we2'], 'L0_ffn_be2': _L0_ffn_in['be2'], 'L0_c': _L0_c, 'L0_wmod': _L0_wmod, 'L1_attn_in_proj_w': _L1_attn_in['in_proj_w'], 'L1_attn_conv_w': _L1_attn_in['conv_w'], 'L1_attn_conv_b': _L1_attn_in['conv_b'], 'L1_attn_w_base': _L1_attn_in['w_base'], 'L1_attn_out_proj_w': _L1_attn_in['out_proj_w'], 'L1_ffn_W_exp': _L1_ffn_in['W_exp'], 'L1_ffn_b_exp': _L1_ffn_in['b_exp'], 'L1_ffn_up_weights': _L1_ffn_in['up_weights'], 'L1_ffn_up_bias': _L1_ffn_in['up_bias'], 'L1_ffn_down_weights': _L1_ffn_in['down_weights'], 'L1_ffn_W_con': _L1_ffn_in['W_con'], 'L1_ffn_b_con': _L1_ffn_in['b_con'], 'L1_ffn_down_bias': _L1_ffn_in['down_bias'], 'L1_c': _L1_c, 'L1_wmod': _L1_wmod}
    _x0 = _d['L0_attn_x']
    _d['L0_attn_x'] = jax.random.normal(jax.random.fold_in(jax.random.key(seed), 1), (8, 256, 128), dtype=_x0.dtype)
    del _x0
    return _d

def reference(L0_attn_x, L0_attn_Wq, L0_attn_bq, L0_attn_Wk, L0_attn_bk, L0_attn_Wv, L0_attn_bv, L0_attn_Wa, L0_attn_ba, L0_attn_Wb, L0_attn_bb, L0_attn_conv_q, L0_attn_conv_k, L0_attn_conv_v, L0_attn_Wo, L0_attn_bo, L0_ffn_rw1, L0_ffn_rb1, L0_ffn_rw2, L0_ffn_rb2, L0_ffn_we1, L0_ffn_be1, L0_ffn_we2, L0_ffn_be2, L0_c, L0_wmod, L1_attn_in_proj_w, L1_attn_conv_w, L1_attn_conv_b, L1_attn_w_base, L1_attn_out_proj_w, L1_ffn_W_exp, L1_ffn_b_exp, L1_ffn_up_weights, L1_ffn_up_bias, L1_ffn_down_weights, L1_ffn_W_con, L1_ffn_b_con, L1_ffn_down_bias, L1_c, L1_wmod):

    def _L0_attn_ref(x, Wq, bq, Wk, bk, Wv, bv, Wa, ba, Wb, bb, conv_q, conv_k, conv_v, Wo, bo):
        import jax, jax.numpy as jnp
        import numpy as np
        DIM = 128
        H = 16
        DH = DIM // H
        K = 4
        B = 8
        N = 256
        EPS = 1e-06

        def _depthwise_conv_silu(x, w, n):
            pad = K // 2
            y = jax.lax.conv_general_dilated(x.transpose(0, 2, 1), w, window_strides=(1,), padding=[(pad, pad)], dimension_numbers=('NCH', 'OIH', 'NCH'), feature_group_count=x.shape[-1])
            y = y[..., :n]
            return jax.nn.silu(y).transpose(0, 2, 1)

        def _l2norm(x):
            return x / (jnp.linalg.norm(x, axis=-1, keepdims=True) + EPS)

        def _forward(x, Wq, bq, Wk, bk, Wv, bv, Wa, ba, Wb, bb, conv_q, conv_k, conv_v, Wo, bo):
            b_, n_, c_ = x.shape
            q = _l2norm(_depthwise_conv_silu(jax.nn.silu(x @ Wq.T + bq), conv_q, n_))
            k = _l2norm(_depthwise_conv_silu(jax.nn.silu(x @ Wk.T + bk), conv_k, n_))
            v = _depthwise_conv_silu(jax.nn.silu(x @ Wv.T + bv), conv_v, n_)
            a = jax.nn.sigmoid(x @ Wa.T + ba)
            bgate = jax.nn.sigmoid(x @ Wb.T + bb)
            q = q.reshape(b_, n_, H, DH).transpose(1, 0, 2, 3)
            k = k.reshape(b_, n_, H, DH).transpose(1, 0, 2, 3)
            v = v.reshape(b_, n_, H, DH).transpose(1, 0, 2, 3)
            a = a.transpose(1, 0, 2)
            bgate = bgate.transpose(1, 0, 2)
            S0 = jnp.zeros((b_, H, DH, DH), x.dtype)

            def step(S, inp):
                qt, kt, vt, at, bt = inp
                at = at[..., None, None]
                bt = bt[..., None, None]
                Sk = jnp.einsum('bhde,bhe->bhd', S, kt)
                outer_Sk_k = Sk[..., :, None] * kt[..., None, :]
                outer_v_k = vt[..., :, None] * kt[..., None, :]
                S_new = at * S - at * bt * outer_Sk_k + bt * outer_v_k
                ot = jnp.einsum('bhd,bhde->bhe', qt, S_new)
                return (S_new, ot)
            _, O = jax.lax.scan(step, S0, (q, k, v, a, bgate))
            O = O.transpose(1, 0, 2, 3).reshape(b_, n_, c_)
            return O @ Wo.T + bo
        return _forward(x, Wq, bq, Wk, bk, Wv, bv, Wa, ba, Wb, bb, conv_q, conv_k, conv_v, Wo, bo)

    def _L0_ffn_ref(x, rw1, rb1, rw2, rb2, we1, be1, we2, be2):
        import jax, jax.numpy as jnp
        import numpy as np
        B, T, D, E, H, K = (2, 256, 128, 8, 512, 2)
        b, t, d = x.shape
        xt = x.reshape(b * t, d)
        n = xt.shape[0]
        logits = jax.nn.silu(xt @ rw1 + rb1) @ rw2 + rb2
        _, idx = jax.lax.top_k(logits, K)
        mask = jnp.zeros((n, E), bool).at[jnp.arange(n)[:, None], idx].set(True)
        w = jax.nn.softmax(jnp.where(mask, logits, -jnp.inf), axis=1)
        h = jax.nn.silu(jnp.einsum('nd,edh->enh', xt, we1) + be1[:, None, :])
        eo = jnp.einsum('enh,ehd->end', h, we2) + be2[:, None, :]
        y = xt + jnp.einsum('ne,end->nd', w, eo)
        return y.reshape(b, t, d)

    def _L1_attn_ref(x, in_proj_w, conv_w, conv_b, w_base, out_proj_w):
        import jax, jax.numpy as jnp
        import numpy as np
        from jax import lax
        B, S, D_MODEL, H, D_CONV, CHUNK = (8, 512, 128, 16, 4, 64)
        D_INNER = D_MODEL

        def _segsum(a):
            T = a.shape[-1]
            lower_strict = jnp.tril(jnp.ones((T, T), bool), -1)
            lower = jnp.tril(jnp.ones((T, T), bool), 0)
            xr = jnp.where(lower_strict, a[..., :, None], 0.0)
            s = jnp.cumsum(xr, axis=-2)
            return jnp.where(lower, s, -jnp.inf)

        def _ssd(x, A, l):
            b, s, h, n = x.shape
            c = s // l
            x = x.reshape(b, c, l, h, n)
            A = A.reshape(b, c, l, h).transpose(0, 3, 1, 2)
            A_cumsum = jnp.cumsum(A, axis=-1)
            L_log = _segsum(A)
            L = jnp.exp(L_log - jnp.max(L_log, axis=-1, keepdims=True))
            norm_diag = L.sum(-1).transpose(0, 2, 3, 1)
            Y_diag = jnp.einsum('bhcls,bcshn->bclhn', L, x)
            decay_states = A_cumsum[..., -1:] - A_cumsum
            decay_states = jnp.exp(decay_states - jnp.max(decay_states, axis=-1, keepdims=True))
            norm_decay = decay_states.sum(-1).transpose(0, 2, 1)
            states = jnp.einsum('bhcl,bclhn->bchn', decay_states, x)
            norm_decay = jnp.pad(norm_decay, ((0, 0), (1, 0), (0, 0)))
            states = jnp.pad(states, ((0, 0), (1, 0), (0, 0), (0, 0)))
            decay_chunk = _segsum(jnp.pad(A_cumsum[..., -1], ((0, 0), (0, 0), (1, 0))))
            decay_chunk = jnp.exp(decay_chunk - jnp.max(decay_chunk, axis=-1, keepdims=True))
            norm_decay = jnp.einsum('bhzc,bch->bzh', decay_chunk, norm_decay)[:, :-1]
            states = jnp.einsum('bhzc,bchn->bzhn', decay_chunk, states)[:, :-1]
            state_decay_out = jnp.exp(A_cumsum - jnp.max(A_cumsum, axis=-1, keepdims=True))
            norm_off = jnp.einsum('bch,bhcl->bclh', norm_decay, state_decay_out)
            Y_off = jnp.einsum('bchn,bhcl->bclhn', states, state_decay_out)
            Y = (Y_diag + Y_off).reshape(b, s, h, n)
            norm = (norm_diag + norm_off).reshape(b, s, h)
            return Y / norm[..., None]
        b, s, d_model = x.shape
        d_inner = in_proj_w.shape[0] - H
        xw = jnp.einsum('bsd,ed->bse', x, in_proj_w)
        xi, w = (xw[..., :d_inner], xw[..., d_inner:])
        xc = lax.conv_general_dilated(xi.transpose(0, 2, 1), conv_w, window_strides=(1,), padding=[(D_CONV - 1, 0)], feature_group_count=d_inner, dimension_numbers=('NCH', 'OIH', 'NCH'))
        xc = (xc + conv_b[None, :, None]).transpose(0, 2, 1)
        xh = xc.reshape(b, s, H, d_inner // H)
        A = w * w_base
        y = _ssd(xh, A, CHUNK)
        y = y.reshape(b, s, d_inner)
        return jnp.einsum('bsd,ed->bse', y, out_proj_w)

    def _L1_ffn_ref(x, W_exp, b_exp, up_weights, up_bias, down_weights, W_con, b_con, down_bias):
        import jax, jax.numpy as jnp
        import numpy as np
        D_MODEL = 128
        EXPANSION = 4
        D_HIDDEN = D_MODEL * EXPANSION
        NUM_STAGES = int(np.log2(D_HIDDEN))

        def butterfly(y, weights, dim):
            lead = y.shape[:-1]
            for stage in range(weights.shape[0]):
                s = 2 ** stage
                nb = dim // (2 * s)
                yr = y.reshape(*lead, nb, 2, s)
                a = yr[..., 0, :]
                b = yr[..., 1, :]
                w = weights[stage].reshape(nb, s, 2, 2)
                na = w[..., 0, 0] * a + w[..., 0, 1] * b
                nb2 = w[..., 1, 0] * a + w[..., 1, 1] * b
                y = jnp.stack([na, nb2], axis=-2).reshape(*lead, dim)
            return y
        h = jnp.einsum('bsd,dh->bsh', x, W_exp) + b_exp
        h = butterfly(h, up_weights, D_HIDDEN)
        h = jax.nn.gelu(h + up_bias, approximate=False)
        h = butterfly(h, down_weights, D_HIDDEN)
        y = jnp.einsum('bsh,hd->bsd', h, W_con) + b_con
        return y + down_bias
    x = L0_attn_x
    mod = (_silu(L0_c) @ L0_wmod).reshape(L0_c.shape[0], 6, 1, -1)
    sa, ca, ga, sb, cb, gb = (mod[:, 0], mod[:, 1], mod[:, 2], mod[:, 3], mod[:, 4], mod[:, 5])
    ga = (2 * (ga >= 0) - 1) * jnp.maximum(jnp.abs(ga), 0.25)
    gb = (2 * (gb >= 0) - 1) * jnp.maximum(jnp.abs(gb), 0.25)
    h = _layernorm(x, axis=-1) * (1 + ca) + sa
    x = x + ga * _L0_attn_ref(h, L0_attn_Wq, L0_attn_bq, L0_attn_Wk, L0_attn_bk, L0_attn_Wv, L0_attn_bv, L0_attn_Wa, L0_attn_ba, L0_attn_Wb, L0_attn_bb, L0_attn_conv_q, L0_attn_conv_k, L0_attn_conv_v, L0_attn_Wo, L0_attn_bo)
    h = _layernorm(x, axis=-1) * (1 + cb) + sb
    x = x + gb * _L0_ffn_ref(h, L0_ffn_rw1, L0_ffn_rb1, L0_ffn_rw2, L0_ffn_rb2, L0_ffn_we1, L0_ffn_be1, L0_ffn_we2, L0_ffn_be2)
    mod = (_silu(L1_c) @ L1_wmod).reshape(L1_c.shape[0], 6, 1, -1)
    sa, ca, ga, sb, cb, gb = (mod[:, 0], mod[:, 1], mod[:, 2], mod[:, 3], mod[:, 4], mod[:, 5])
    ga = (2 * (ga >= 0) - 1) * jnp.maximum(jnp.abs(ga), 0.25)
    gb = (2 * (gb >= 0) - 1) * jnp.maximum(jnp.abs(gb), 0.25)
    h = _layernorm(x, axis=-1) * (1 + ca) + sa
    x = x + ga * _L1_attn_ref(h, L1_attn_in_proj_w, L1_attn_conv_w, L1_attn_conv_b, L1_attn_w_base, L1_attn_out_proj_w)
    h = _layernorm(x, axis=-1) * (1 + cb) + sb
    x = x + gb * _L1_ffn_ref(h, L1_ffn_W_exp, L1_ffn_b_exp, L1_ffn_up_weights, L1_ffn_up_bias, L1_ffn_down_weights, L1_ffn_W_con, L1_ffn_b_con, L1_ffn_down_bias)
    return x

_drawn_inputs = setup_inputs


def setup_inputs(seed=0):
    import zlib

    import numpy as np

    out = dict(_drawn_inputs(seed))
    spreads = {'L0_attn_bq': (0.0, 0.8),
     'L0_attn_bk': (0.0, 0.8),
     'L0_attn_bv': (0.0, 0.8),
     'L0_attn_ba': (0.0, 0.8),
     'L0_attn_bb': (0.0, 0.8),
     'L0_attn_bo': (0.0, 0.324),
     'L0_ffn_rb1': (0.0, 0.8),
     'L0_ffn_rb2': (0.0, 0.397),
     'L0_ffn_be1': (0.0, 0.8),
     'L0_ffn_be2': (0.0, 0.496),
     'L1_attn_conv_b': (0.0, 0.8),
     'L1_ffn_b_exp': (0.0, 0.1),
     'L1_ffn_up_bias': (0.0, 0.1),
     'L1_ffn_b_con': (0.0, 1.364),
     'L1_ffn_down_bias': (0.0, 1.518)}
    factors = {'L0_attn_Wq': 8.0,
     'L0_attn_Wk': 8.0,
     'L0_attn_Wv': 8.0,
     'L0_attn_Wa': 8.0,
     'L0_attn_Wb': 8.0,
     'L0_attn_conv_q': 8.0,
     'L0_attn_conv_k': 8.0,
     'L0_attn_conv_v': 8.0,
     'L0_attn_Wo': 8.0,
     'L0_ffn_rw1': 5.151,
     'L0_ffn_rw2': 5.399,
     'L0_ffn_we1': 6.324,
     'L0_ffn_we2': 5.677,
     'L1_attn_in_proj_w': 8.0,
     'L1_attn_conv_w': 8.0,
     'L1_attn_w_base': 8.0,
     'L1_attn_out_proj_w': 8.0}
    for name, (base, spread) in spreads.items():
        noise = np.random.default_rng([zlib.crc32(name.encode()), seed]).standard_normal(out[name].shape)
        drawn = base * np.exp(spread * noise) if base else spread * noise
        out[name] = jnp.asarray(drawn.astype(out[name].dtype))
    for name, factor in factors.items():
        out[name] = (out[name] * factor).astype(out[name].dtype)
    return out
```

```python
from contextlib import ExitStack

import numpy as np
import concourse.bass as bass
from concourse import mybir
from concourse.alu_op_type import AluOpType as ALU

P = 128
NB, SEQ = 8, 256
HEADS, DH = 16, 8
WINDOWS = 4
TW = SEQ // WINDOWS
COLS = NB * TW
CH = 8
NCH = TW // CH
BC = NB * NCH
TAPS = 4
EXPERTS, HID = 8, 512
HT = HID // P
TT = COLS // P
STAGES = 9
BIG = 1.0e30
fp32 = mybir.dt.float32
ACT = mybir.ActivationFunctionType
AX = mybir.AxisListType

_w = [("bq", 1), ("bk", 1), ("bv", 1), ("ba", 1), ("bb", 1), ("bo", 1), ("rb1", 1),
      ("cq", TAPS), ("ck", TAPS), ("cv", TAPS), ("cx", TAPS), ("cb", 1), ("wbase", 1),
      ("be1", EXPERTS * HT), ("upb", HT), ("bcon", 1), ("downb", 1)]
COL, _n = {}, 0
for _name, _k in _w:
    COL[_name] = _n
    _n += _k
NCOL = _n
MATS = ["wq", "wk", "wv", "wa", "wb", "rw1", "win", "wdec", "wout"]
CONSTS = ["center", "mean", "headones", "ident"]
SA, CA, GA, SB, CB, GB = range(6)
PACK = [(0, 6), (1, 5), (2, 4), (3,)]


def program(nc, xT, mats, consts, cols, cT, wmod, wo_rep, rw2, rb2, be2, we1, we2, lower, w_exp, b_exp,
            w_conT, up_coef, down_coef, scratch, outT):
    ctx = ExitStack()
    with ctx:
        def sb(name, *shape):
            return ctx.enter_context(nc.sbuf_tensor(name, list(shape), fp32))

        def sem(name):
            return ctx.enter_context(nc.semaphore(name))

        x = sb("x", P, WINDOWS, COLS)
        M = sb("M", P, len(MATS), P)
        C = sb("C", P, len(CONSTS), P)
        col = sb("col", P, NCOL)
        csil = sb("csil", P, 2, NB)
        eps = sb("eps", P, 1)
        mod = sb("mod", P, 12, NB)
        gsg = sb("gsg", P, 4, NB)
        gab = sb("gab", P, 4, NB)
        worep = sb("worep", P, DH, P)
        rw2s = sb("rw2s", P, EXPERTS)
        rb2s = sb("rb2s", P, EXPERTS)
        be2s = sb("be2s", EXPERTS, P)
        we1s = sb("we1s", P, EXPERTS, HID)
        we2s = sb("we2s", P, EXPERTS, HT, P)
        low = sb("low", P, EXPERTS, EXPERTS)
        sq = sb("sq", P, COLS)
        rs = sq
        hf = sb("hf", P, NB, SEQ)
        h2 = sb("h", P, COLS)
        h3 = h4 = h2
        HALO = TAPS - 1
        p = sb("p", P, 3, NB, TW + HALO)
        ag = sb("ag", P, COLS)
        bg = sb("bg", P, COLS)
        G = [sb(f"G{j}", P, BC, CH - j) for j in range(CH)]
        Mj = [G[j][:, :, 1:] for j in range(CH - 1)]
        XK = sb("XK", P, COLS)
        cpd = XK
        krep = sb("krep", P, DH, COLS)
        wrep = sb("wrep", P, DH, COLS)
        wm = wrep[:, 0:3, :].rearrange("p a n -> p (a n)").rearrange("p (l n) -> p l n", l=2)
        A9 = [sb(f"A9{i}", P, NB * DH, CH + 1) for i in range(2)]
        R = sb("R", P, NB, CH)
        U = sb("U", P, NB, CH)
        D1 = sb("D1", P, NB * DH, CH + 1)
        NH_ = 3
        H = [sb(f"H{i}", P, NB * DH, CH + 1) for i in range(NH_)]
        QS = sb("QS", P, DH, COLS)
        br = sb("br", P, COLS)

        work = sb("work", P, 10, COLS)
        c3 = y = work[:, 0:3, :]
        KK = work[:, 3:7, :]
        sq2 = work[:, 3:5, :]
        nrm = work[:, 5:7, :]
        qn, kn, XV = (work[:, i, :] for i in range(3))
        kb = work[:, 7, :]
        tk = work[:, 8, :]
        tv = work[:, 9, :]
        Pb = work[:, 7, :].rearrange("p (b e i) -> p b e i", b=NB, e=DH)
        r1 = work[:, 3, :]
        gt = work[:, 4, 0:TT * EXPERTS * EXPERTS].rearrange("p (t a b) -> p t a b", t=TT, a=EXPERTS)
        eq = work[:, 4, TT * EXPERTS * EXPERTS:].rearrange("p (t a b) -> p t a b", t=TT, a=EXPERTS)
        gateT = work[0:EXPERTS, 5, :].rearrange("p (t n) -> p t n", t=TT)
        xc, A, ge = work[:, 0, :], work[:, 1, :], work[:, 2, :]
        gd, gx = ge, xc

        def timed(i):
            return work[:, i, :].rearrange("p (b t) -> p b t", b=NB)
        ac, rm, Y, N, so, yo, no = (timed(i) for i in range(3, 10))
        sde = so
        lg = sb("lg", P, TT, EXPERTS)
        rank = sb("rank", P, TT, EXPERTS)
        lmax = sb("lmax", P, TT)
        ls = sb("ls", P, TT, EXPERTS)
        ex = ls
        exm = sb("exm", P, TT, EXPERTS)
        den = sb("den", P, TT)
        rden = sb("rden", P, TT)
        gate = sb("gate", P, TT, EXPERTS)
        hidb = sb("hid", P, 2 * HT, COLS)
        hid = [hidb[:, i * HT:(i + 1) * HT, :] for i in range(2)]
        cmbb = sb("cmb", P, 2, COLS)
        cmb = [cmbb[:, i, :].rearrange("p (t n) -> p t n", t=TT) for i in range(2)]
        acc = sb("acc", P, TT, P)
        xi = sb("xi", P, NB, TW + HALO)
        segm = sb("segm", P, NB, TW)
        segb = sb("segb", P, NB, TW)
        EE = sb("EE", P, NB, TW)
        dm = EE
        mx = sb("mx", P, NB)
        Ms = [sb(f"Ms{i}", P, NB) for i in range(2)]
        t8 = sb("t8", P, 2, NB)
        f8 = sb("f8", P, 2, NB)
        Hs = sb("Hs", P, 2, NB)
        Yl = sb("Yl", P, 2, NB)
        wx = sb("wx", P, HID)
        wc = sb("wc", P, HID)
        coef = [hidb[:, 2 * i:2 * i + 2, :] for i in range(2)]
        ft = hidb[:, 4:6, :]
        bx = hidb[0:1, 6, :]
        fb = cmbb[0:1, :, :]
        ubias = sb("ubias", P, HT)
        dbias = sb("dbias", P, 1)
        wcT = wc[:, :].rearrange("p (t n) -> p t n", t=HT)
        u = hidb[:, 0:HT, :]

        s_x0_in = sem("x0_in")
        s_const_in = sem("const_in")
        s_mod_in = sem("mod_in")
        s_col_in = sem("col_in")
        s_mat_in = sem("mat_in")
        s_x_in = sem("x_in")
        s_fold_in = sem("fold_in")
        s_exp_in = sem("exp_in")
        s_we1_in = sem("we1_in")
        s_we2_in = sem("we2_in")
        s_fold_off = sem("fold_off")
        s_bfold_off = sem("bfold_off")
        s_coef_in = [sem(f"coef_in{i}") for i in range(2)]
        s_mod_mm = sem("mod_mm")
        s_kn_done = sem("kn_done")
        s_kn_out = sem("kn_out")
        s_outer_done = sem("outer_done")
        s_krep_in = sem("krep_in")
        s_xk_sub = sem("xk_sub")
        s_xk_out = sem("xk_out")
        s_prod_done = sem("prod_done")
        s_wrep_in = sem("wrep_in")
        s_x4_done = sem("x4_done")
        s_stored = sem("stored")
        s_ln_n1 = sem("ln_n1")
        s_ln_c = sem("ln_c")
        s_ln_sq = sem("ln_sq")
        s_ln_v = sem("ln_v")
        s_csil_done = sem("csil_done")
        s_ln_h = sem("ln_h")
        s_mod_read = sem("mod_read")
        s_proj0_mm = sem("proj0_mm")
        s_u_done = sem("u_done")
        s_ffn_read = sem("ffn_read")
        s_cmb_done = sem("cmb_done")
        s_acc0_done = sem("acc0_done")
        s_lgT_read = sem("lgT_read")
        s_proj_mm = sem("proj_mm")
        s_l2_sq = sem("l2_sq")
        s_gates_done = sem("gates_done")
        s_p_done = sem("p_done")
        s_l2_mm = sem("l2_mm")
        s_kk_done = sem("kk_done")
        s_l2_root = sem("l2_root")
        s_mj_done = sem("mj_done")
        s_kk_mm = sem("kk_mm")
        s_qs_done = sem("qs_done")
        s_ub_done = sem("ub_done")
        s_zo_done = sem("zo_done")
        s_attn_mm = sem("attn_mm")
        s_r1_mm = sem("r1_mm")
        s_r1_done = sem("r1_done")
        s_lg_mm = sem("lg_mm")
        s_gate_done = sem("gate_done")
        s_gT_mm = sem("gT_mm")
        s_acc0_mm = sem("acc0_mm")
        s_hid_done = sem("hid_done")
        s_hid_mm = sem("hid_mm")
        s_eo_mm = sem("eo_mm")
        s_acc_done = sem("acc_done")
        s_yT_mm = sem("yT_mm")
        s_in_mm = sem("in_mm")
        s_yf_done = sem("yf_done")
        s_dec_mm = sem("dec_mm")
        s_yn_done = sem("yn_done")
        s_out_mm = sem("out_mm")
        s_bfold_sum = sem("bfold_sum")
        s_ub_mm = sem("ub_mm")
        s_fold_sum = sem("fold_sum")
        s_a_raw = sem("a_raw")
        s_wcT_mm = sem("wcT_mm")
        s_u_mm = sem("u_mm")
        s_wcT_done = sem("wcT_done")
        s_ffn_mm = sem("ffn_mm")
        s_x1_done = sem("x1_done")
        s_x2_done = sem("x2_done")
        s_x3_done = sem("x3_done")
        s_ln_sd = sem("ln_sd")
        s_carry_done = sem("carry_done")
        s_xk_init = sem("xk_init")
        s_conv_tap = sem("conv_tap")
        s_c3_done = sem("c3_done")
        s_scan_done = sem("scan_done")
        s_a9_done = sem("a9_done")
        s_ao_done = sem("ao_done")
        s_ls_done = sem("ls_done")
        s_ex_done = sem("ex_done")
        s_halo_done = sem("halo_done")
        s_xi_done = sem("xi_done")
        s_ac_done = sem("ac_done")
        s_dm_done = sem("dm_done")
        s_n_done = sem("n_done")
        s_ee_done = sem("ee_done")
        s_gd_done = sem("gd_done")
        s_ge_done = sem("ge_done")
        s_so_done = sem("so_done")
        s_no_done = sem("no_done")
        s_sde_done = sem("sde_done")
        s_t8_done = sem("t8_done")
        s_f8_done = sem("f8_done")
        s_eps_set = sem("eps_set")
        s_set = sem("set")
        s_ln_rs = sem("ln_rs")
        s_mod_scale = sem("mod_scale")
        s_mod_sign = sem("mod_sign")
        s_mod_neg = sem("mod_neg")
        s_mod_abs = sem("mod_abs")
        s_mod_done = sem("mod_done")
        s_bfold_diag = sem("bfold_diag")
        s_pad_set = sem("pad_set")
        s_l2_eps = sem("l2_eps")
        s_l2_rn = sem("l2_rn")
        s_g_done = sem("g_done")
        s_cp_done = sem("cp_done")
        s_xk_prod = sem("xk_prod")
        s_xv_sub = sem("xv_sub")
        s_seed_done = sem("seed_done")
        s_red_done = sem("red_done")
        s_u_delta = sem("u_delta")
        s_route_q = sem("route_q")
        s_lg_done = sem("lg_done")
        s_lmax_done = sem("lmax_done")
        s_cmp_done = sem("cmp_done")
        s_rank_done = sem("rank_done")
        s_exm_done = sem("exm_done")
        s_den_done = sem("den_done")
        s_rden_done = sem("rden_done")
        s_xc_tap = sem("xc_tap")
        s_rm_done = sem("rm_done")
        s_mx_done = sem("mx_done")
        s_t8_a = sem("t8_a")
        s_ms_done = sem("ms_done")
        s_t8_n = sem("t8_n")
        s_gx_done = sem("gx_done")
        s_nd_done = sem("nd_done")
        s_hs_done = sem("hs_done")
        s_nt_done = sem("nt_done")
        s_yt_done = sem("yt_done")
        s_rN_done = sem("rN_done")
        s_hs_a = sem("hs_a")
        s_ln_n2 = sem("ln_n2")
        s_vb_done0 = sem("vb_done0")
        s_qn_done = sem("qn_done")
        s_kb_done = sem("kb_done")
        s_xv_prod = sem("xv_prod")
        s_fold_diag = sem("fold_diag")
        s_g_set = sem("g_set")
        s_aog_done = sem("aog_done")
        s_yg_done = sem("yg_done")
        s_y4_done = sem("y4_done")

        def pb(name, *shape):
            return ctx.enter_context(nc.psum_tensor(name, list(shape), fp32))
        psA = pb("psA", P, COLS)
        psB = pb("psB", P, COLS)
        psF = [pb(f"psF{i}", P, COLS) for i in range(2)]
        psS = [pb(f"psS{i}", P, COLS) for i in range(2)]
        psM = pb("psM", P, 2, COLS)

        def m(name):
            return M[:, MATS.index(name), :]

        def cst(name):
            return C[:, CONSTS.index(name), :]

        def pc(name, i=0):
            return col[:, COL[name] + i:COL[name] + i + 1]

        def bt(ap):
            return ap.rearrange("p (b t) -> p b t", b=NB)

        def bci(ap):
            return ap.rearrange("p (g i) -> p g i", i=CH)

        def per_b(i, l=0):
            return mod[:, 6 * l + i, :].unsqueeze(2).broadcast_to([P, NB, TW])

        def ln_front(w):
            return w

        def ln_of(k, w):
            return WINDOWS + 3 * w + k

        block = ctx.enter_context(nc.Block())

        @block.sync
        def _(sp):
            sp.dma_start(x[:, 0, :], xT[:, 0, :]).then_inc(s_x0_in, 16)
            sp.dma_start(C[:, :, :], consts).then_inc(s_const_in, 16)
            sp.dma_start(csil[:, :, :], cT).then_inc(s_mod_in, 16)
            sp.dma_start(wm[:, :, :], wmod).then_inc(s_mod_in, 16)
            sp.dma_start(col[:, :], cols).then_inc(s_col_in, 16)
            sp.dma_start(M[:, :, :], mats).then_inc(s_mat_in, 16)
            for w in range(1, WINDOWS):
                sp.dma_start(x[:, w, :], xT[:, w, :]).then_inc(s_x_in, 16)
            sp.dma_start(bx[:, :], b_exp).then_inc(s_fold_in, 16)
            sp.dma_start(wx[:, :], w_exp).then_inc(s_fold_in, 16)
            sp.dma_start(wc[:, :], w_conT).then_inc(s_fold_in, 16)
            sp.dma_start(worep[:, :, :], wo_rep).then_inc(s_exp_in, 16)
            sp.dma_start(rw2s[:, :], rw2).then_inc(s_exp_in, 16)
            sp.dma_start(rb2s[:, :], rb2.partition_broadcast(P)).then_inc(s_exp_in, 16)
            sp.dma_start(be2s[:, :], be2).then_inc(s_exp_in, 16)
            sp.dma_start(low[:, :, :], lower.partition_broadcast(P)).then_inc(s_exp_in, 16)
            sp.dma_start(we1s[:, :, :], we1).then_inc(s_we1_in, 16)
            sp.dma_start(we2s[:, :, :, :], we2).then_inc(s_we2_in, 16)

            def fold_load(s):
                src, i = (up_coef, s) if s < STAGES else (down_coef, s - STAGES)
                if s >= 2:
                    sp.wait_ge(s_fold_off, 2 * (s - 1))
                    sp.wait_ge(s_bfold_off, 2 * min(s - 1, STAGES))
                sp.dma_start(coef[s % 2][:, :, :], src[i].partition_broadcast(P)).then_inc(s_coef_in[s % 2], 16)

            def spread_keys(w):
                sp.wait_ge(s_mod_mm, 1)
                sp.wait_ge(s_kn_done, w + 1)
                sp.dma_start(scratch[w, 0, :, :], kn[:, :]).then_inc(s_kn_out, 16)
                sp.wait_ge(s_kn_out, 16 * (w + 1))
                if NCH * w > 0:
                    sp.wait_ge(s_outer_done, NCH * w)
                for d in range(DH):
                    sp.dma_start(krep[d::DH, :, :], scratch[w, 0, :, :].rearrange("(h e) n -> h e n", e=DH)).then_inc(s_krep_in, 16)

            def spread_solved(w):
                sp.wait_ge(s_xk_sub, (CH - 1) * (w + 1))
                sp.dma_start(scratch[w, 1, :, :], XK[:, :]).then_inc(s_xk_out, 16)
                sp.wait_ge(s_xk_out, 16 * (w + 1))
                if NCH * w > 0:
                    sp.wait_ge(s_prod_done, NCH * w)
                for d in range(DH):
                    sp.dma_start(wrep[d::DH, :, :], scratch[w, 1, :, :].rearrange("(h e) n -> h e n", e=DH)).then_inc(s_wrep_in, 16)

            fold_load(0)
            fold_load(1)
            for w in range(WINDOWS):
                spread_keys(w)
                spread_solved(w)
                if w == 0:
                    for s in range(2, 2 * STAGES):
                        fold_load(s)
                if w > 0:
                    sp.wait_ge(s_x4_done, w)
                    sp.dma_start(outT[:, w - 1, :], x[:, w - 1, :]).then_inc(s_stored, 16)
            sp.wait_ge(s_x4_done, WINDOWS)
            sp.dma_start(outT[:, WINDOWS - 1, :], x[:, WINDOWS - 1, :]).then_inc(s_stored, 16)
            sp.wait_ge(s_stored, 16 * WINDOWS)

        @block.tensor
        def _(pe):
            mm = nc.tensor.matmul

            def ln(n, src):
                if n > 0:
                    pe.wait_ge(s_ln_n1, n)
                mm(psA[:, :], cst("center"), src, start=True, stop=True).then_inc(s_ln_c, 1)
                pe.wait_ge(s_ln_sq, n + 1)
                mm(psB[:, :], cst("mean"), sq[:, :], start=True, stop=True).then_inc(s_ln_v, 1)

            def modulation():
                pe.wait_ge(s_csil_done, 1)
                for l in range(2):
                    for i in range(6):
                        last = mm(psM[:, 0, (6 * l + i) * NB:(6 * l + i + 1) * NB], wm[:, l, i * P:(i + 1) * P],
                                  csil[:, l, :], start=True, stop=True)
                last.then_inc(s_mod_mm, 1)

            def pre(w):
                if w == 0:
                    pe.wait_ge(s_ln_h, WINDOWS)
                    pe.wait_ge(s_mod_read, 1)
                    for i, name in enumerate(["wq", "wk", "wv"]):
                        last = mm(psM[:, 0, i * NB:(i + 1) * NB], m(name), hf[:, :, 0:1], start=True, stop=True)
                    last.then_inc(s_proj0_mm, 1)
                else:
                    if HT * (w - 1) > 0:
                        pe.wait_ge(s_u_done, HT * (w - 1))
                    if w - 1 > 0:
                        pe.wait_ge(s_ffn_read, w - 1)
                    if TT * EXPERTS * (w - 1) > 0:
                        pe.wait_ge(s_cmb_done, TT * EXPERTS * (w - 1))
                    pe.wait_ge(s_acc0_done, w)
                    pe.wait_ge(s_lgT_read, w)
                n = TW if w + 1 < WINDOWS else TW - 1
                bank = [psF[0][:, :], psF[1][:, :], psS[0][:, :]]
                for i, name in enumerate(["wq", "wk", "wv"]):
                    mm(bank[i][:, 0:NB * n], m(name), hf[:, :, w * TW + 1:w * TW + 1 + n], start=True,
                       stop=True).then_inc(s_proj_mm, 1)
                for name, bank in (("wa", psS[1][:, :]), ("wb", psM[:, 1, :])):
                    mm(bank, m(name), hf[:, :, w * TW:(w + 1) * TW], start=True, stop=True).then_inc(s_proj_mm, 1)
                pe.wait_ge(s_l2_sq, w + 1)
                pe.wait_ge(s_gates_done, 2 * (w + 1))
                pe.wait_ge(s_p_done, 3 * w + 4)
                for i in range(2):
                    mm(psM[:, i, :], cst("mean"), sq2[:, i, :], start=True, stop=True).then_inc(s_l2_mm, 1)
                for g, js in enumerate(PACK):
                    pe.wait_ge(s_kk_done, 7 * w + sum(len(q) for q in PACK[:g + 1]))
                    if g < 2:
                        pe.wait_ge(s_l2_root, w + 1)
                    else:
                        pe.wait_ge(s_mj_done, 7 * w + sum(len(q) for q in PACK[:g - 1]))
                    n = sum((CH - 1 - j) * BC for j in js)
                    mm(psM[:, g % 2, 0:n], cst("headones"), KK[:, g, 0:n], start=True, stop=True).then_inc(s_kk_mm, 1)

            def attn_out(w):
                pe.wait_ge(s_qs_done, NCH * (w + 1))
                if w == 0:
                    pe.wait_ge(s_ub_done, 2)
                if w > 0:
                    pe.wait_ge(s_zo_done, w)
                pe.wait_ge(s_mj_done, 7 * (w + 1))
                for e in range(DH):
                    last = mm(psM[:, 0, :], worep[:, e, :], QS[:, e, :], start=(e == 0), stop=(e == DH - 1))
                last.then_inc(s_attn_mm, 1)

            def router(w):
                pe.wait_ge(s_ln_h, ln_of(0, w) + 1)
                mm(psM[:, 1, :], m("rw1"), h2[:, :], start=True, stop=True).then_inc(s_r1_mm, 1)
                pe.wait_ge(s_r1_done, w + 1)
                for t in range(TT):
                    last = mm(psM[:, 0, t * EXPERTS:(t + 1) * EXPERTS], r1[:, t * P:(t + 1) * P], rw2s[:, :],
                              start=True, stop=True)
                last.then_inc(s_lg_mm, 1)

            def router_bias(w):
                pe.wait_ge(s_gate_done, w + 1)
                for t in range(TT):
                    last = nc.tensor.transpose(psM[0:EXPERTS, 1, t * P:(t + 1) * P], gate[:, t, :], cst("ident"))
                last.then_inc(s_gT_mm, 1)
                pe.wait_ge(s_lgT_read, w + 1)
                for t in range(TT):
                    last = mm(psM[:, 0, t * P:(t + 1) * P], gateT[:, t, :], be2s[:, :], start=True, stop=True)
                last.then_inc(s_acc0_mm, 1)

            def experts(w):
                def first(e):
                    for k in range(HT):
                        n = HT * (EXPERTS * w + e) + k
                        if n - 1 > 0:
                            pe.wait_ge(s_hid_done, n - 1)
                        if w > 0 and e == 0:
                            pe.wait_ge(s_u_done, HT * w)
                        mm(psF[n % 2][:, :], we1s[:, e, k * P:(k + 1) * P], h2[:, :], start=True,
                           stop=True).then_inc(s_hid_mm, 1)

                def second(e):
                    n = EXPERTS * w + e
                    pe.wait_ge(s_hid_done, HT * (n + 1))
                    if TT * (n - 1) > 0:
                        pe.wait_ge(s_cmb_done, TT * (n - 1))
                    if w > 0 and e == 0:
                        pe.wait_ge(s_ffn_read, w)
                    for t in range(TT):
                        for k in range(HT):
                            last = mm(psS[n % 2][:, t * P:(t + 1) * P], hid[n % 2][:, k, t * P:(t + 1) * P],
                                      we2s[:, e, k, :], start=(k == 0), stop=(k == HT - 1))
                    last.then_inc(s_eo_mm, 1)

                if w + 1 < WINDOWS:
                    pe.wait_ge(s_p_done, 1 + 3 * (w + 2))
                    pe.wait_ge(s_gates_done, 2 * (w + 2))
                first(0)
                for e in range(1, EXPERTS):
                    first(e)
                    second(e - 1)
                second(EXPERTS - 1)
                pe.wait_ge(s_acc_done, EXPERTS * (w + 1))
                pe.wait_ge(s_mj_done, 7 * min(w + 2, WINDOWS))
                for t in range(TT):
                    last = nc.tensor.transpose(psM[:, 1, t * P:(t + 1) * P], acc[:, t, :], cst("ident"))
                last.then_inc(s_yT_mm, 1)

            def ssd(w):
                pe.wait_ge(s_ln_h, ln_of(1, w) + 1)
                mm(psM[:, 0, :], m("win"), h3[:, :], start=True, stop=True).then_inc(s_in_mm, 1)
                pe.wait_ge(s_yf_done, w + 1)
                mm(psM[:, 1, :], m("wdec"), h3[:, :], start=True, stop=True).then_inc(s_dec_mm, 1)
                pe.wait_ge(s_yn_done, w + 1)
                mm(psM[:, 0, :], m("wout"), yo[:, :, :].rearrange("p b t -> p (b t)"), start=True,
                   stop=True).then_inc(s_out_mm, 1)

            def fold_bias():
                pe.wait_ge(s_bfold_sum, STAGES)
                pe.wait_ge(s_mj_done, 7)
                for k in range(HT):
                    last = mm(psM[:, 0, k:k + 1], bx[0:1, k * P:(k + 1) * P], cst("ident")[0:1, 0:1], start=True, stop=True)
                last.then_inc(s_ub_mm, 1)

            def fold_down():
                pe.wait_ge(s_fold_sum, 2 * STAGES)
                pe.wait_ge(s_a_raw, 1)
                for k in range(HT):
                    last = nc.tensor.transpose(psM[:, 1, k * P:(k + 1) * P], wc[:, k * P:(k + 1) * P], cst("ident"))
                last.then_inc(s_wcT_mm, 1)

            def ffn(w):
                pe.wait_ge(s_ln_h, ln_of(2, w) + 1)
                for k in range(HT):
                    if HT * w + k - 1 > 0:
                        pe.wait_ge(s_u_done, HT * w + k - 1)
                    mm(psF[k % 2][:, :], wx[:, k * P:(k + 1) * P], h4[:, :], start=True, stop=True).then_inc(s_u_mm, 1)
                if w == 0:
                    pe.wait_ge(s_wcT_done, 1)
                for k in range(HT):
                    pe.wait_ge(s_u_done, HT * w + k + 1)
                    last = mm(psS[0][:, :], wcT[:, k, :], u[:, k, :], start=(k == 0), stop=(k == HT - 1))
                last.then_inc(s_ffn_mm, 1)

            pe.wait_ge(s_const_in, 16)
            pe.wait_ge(s_x0_in, 16)
            ln(0, x[:, 0, :])
            modulation()
            pe.wait_ge(s_x_in, 16 * (WINDOWS - 1))
            for w in range(1, WINDOWS):
                ln(ln_front(w), x[:, w, :])
            pe.wait_ge(s_mat_in, 16)
            pre(0)
            fold_bias()
            for w in range(WINDOWS):
                if w == 0:
                    pe.wait_ge(s_exp_in, 16 * 5)
                attn_out(w)
                pe.wait_ge(s_x1_done, w + 1)
                ln(ln_of(0, w), x[:, w, :])
                router(w)
                router_bias(w)
                if w + 1 < WINDOWS:
                    pre(w + 1)
                if w == 0:
                    pe.wait_ge(s_we1_in, 16)
                    pe.wait_ge(s_we2_in, 16)
                experts(w)
                pe.wait_ge(s_x2_done, w + 1)
                ln(ln_of(1, w), x[:, w, :])
                ssd(w)
                if w == 0:
                    fold_down()
                pe.wait_ge(s_x3_done, w + 1)
                ln(ln_of(2, w), x[:, w, :])
                ffn(w)

        @block.scalar
        def _(act):
            def ln(n):
                act.wait_ge(s_ln_c, n + 1)
                nc.scalar.activation(sq[:, :], psA[:, :], ACT.Square).then_inc(s_ln_sq, 1)
                act.wait_ge(s_ln_v, n + 1)
                if n > 0:
                    act.wait_ge(s_ln_n1, n)
                nc.scalar.activation(rs[:, :], psB[:, :], ACT.Sqrt, bias=eps[:, 0:1]).then_inc(s_ln_sd, 1)

            def pre(w):
                act.wait_ge(s_carry_done, w + 1)
                n = TW if w + 1 < WINDOWS else TW - 1
                if w == 0:
                    act.wait_ge(s_proj0_mm, 1)
                    b = psM[:, 0, 0:3 * NB].rearrange("p (i b) -> p i b", i=3)
                    for i, name in enumerate(["bq", "bk", "bv"]):
                        last = nc.scalar.activation(p[:, i, :, HALO - 1], b[:, i, :], ACT.Silu, bias=pc(name))
                    last.then_inc(s_p_done, 1)
                for i, (b, name) in enumerate(zip([psF[0], psF[1], psS[0]], ["bq", "bk", "bv"])):
                    act.wait_ge(s_proj_mm, 5 * w + i + 1)
                    nc.scalar.activation(p[:, i, :, HALO:HALO + n], b[:, 0:NB * n].rearrange("p (b t) -> p b t", b=NB), ACT.Silu, bias=pc(name)).then_inc(s_p_done, 1)
                act.wait_ge(s_proj_mm, 5 * w + 5)
                if w > 0:
                    act.wait_ge(s_xk_init, w)
                nc.scalar.activation(ag[:, :], psS[1][:, :], ACT.Sigmoid, bias=pc("ba")).then_inc(s_gates_done, 1)
                nc.scalar.activation(bg[:, :], psM[:, 1, :], ACT.Sigmoid, bias=pc("bb")).then_inc(s_gates_done, 1)
                act.wait_ge(s_conv_tap, 3 * TAPS * (w + 1))
                nc.scalar.activation(c3[:, :, :], y[:, :, :], ACT.Silu).then_inc(s_c3_done, 1)
                act.wait_ge(s_c3_done, w + 1)
                nc.scalar.activation(sq2[:, :, :], c3[:, 0:2, :], ACT.Square).then_inc(s_l2_sq, 1)
                act.wait_ge(s_l2_mm, 2 * (w + 1))
                nc.scalar.activation(nrm[:, :, :], psM[:, :, :], ACT.Sqrt, scale=float(P)).then_inc(s_l2_root, 1)
                act.wait_ge(s_gates_done, 2 * (w + 1))
                decays(w, 0)
                decays(w, 1)

            def decays(w, c):
                g = NCH * w + c
                if g - 1 > 0:
                    act.wait_ge(s_scan_done, g - 1)
                a = bt(ag[:, :])[:, :, c * CH:(c + 1) * CH].unsqueeze(2).broadcast_to([P, NB, DH, CH])
                nc.scalar.activation(A9[g % 2][:, :, 1:CH + 1].rearrange("p (b e) i -> p b e i", b=NB), a, ACT.Copy).then_inc(s_a9_done, 1)

            def router(w):
                act.wait_ge(s_attn_mm, w + 1)
                if w > 0:
                    act.wait_ge(s_x4_done, w)
                nc.scalar.activation(br[:, :], psM[:, 0, :], ACT.Identity, bias=pc("bo")).then_inc(s_ao_done, 1)
                ln(ln_of(0, w))
                act.wait_ge(s_r1_mm, w + 1)
                if w > 0:
                    act.wait_ge(s_lg_mm, w)
                nc.scalar.activation(r1[:, :], psM[:, 1, :], ACT.Silu, bias=pc("rb1")).then_inc(s_r1_done, 1)
                act.wait_ge(s_ls_done, w + 1)
                nc.scalar.activation(ex[:, :, :], ls[:, :, :], ACT.Exp).then_inc(s_ex_done, 1)
                act.wait_ge(s_gT_mm, w + 1)
                if w > 0:
                    act.wait_ge(s_acc0_mm, w)
                nc.scalar.activation(gateT[:, :, :], psM[0:EXPERTS, 1, :].rearrange("e (t n) -> e t n", t=TT), ACT.Copy).then_inc(s_lgT_read, 1)
                act.wait_ge(s_acc0_mm, w + 1)
                if w > 0:
                    act.wait_ge(s_yT_mm, w)
                nc.scalar.activation(acc[:, :, :], psM[:, 0, :].rearrange("p (t n) -> p t n", t=TT), ACT.Copy).then_inc(s_acc0_done, 1)

            def experts(w):
                def hidden(e):
                    for k in range(HT):
                        n = HT * (EXPERTS * w + e) + k
                        act.wait_ge(s_hid_mm, n + 1)
                        if EXPERTS * w + e - 1 > 0:
                            act.wait_ge(s_eo_mm, EXPERTS * w + e - 1)
                        nc.scalar.activation(hid[(EXPERTS * w + e) % 2][:, k, :], psF[n % 2][:, :], ACT.Silu,
                          bias=pc("be1", HT * e + k)).then_inc(s_hid_done, 1)

                def combine(e):
                    n = EXPERTS * w + e
                    act.wait_ge(s_eo_mm, n + 1)
                    if n - 1 > 0:
                        act.wait_ge(s_acc_done, n - 1)
                    for t in range(TT):
                        nc.scalar.activation(cmb[n % 2][:, t, :], psS[n % 2][:, t * P:(t + 1) * P], ACT.Copy,
                          scale=gate[:, t, e:e + 1]).then_inc(s_cmb_done, 1)
                if w == 0:
                    act.wait_ge(s_fold_sum, 2 * STAGES)
                    act.wait_ge(s_ub_mm, 1)
                hidden(0)
                for e in range(1, EXPERTS):
                    hidden(e)
                    combine(e - 1)
                    if w + 1 < WINDOWS and e + 1 < NCH:
                        decays(w + 1, e + 1)
                combine(EXPERTS - 1)

            def ssd(w):
                ln(ln_of(1, w))
                act.wait_ge(s_in_mm, w + 1)
                act.wait_ge(s_halo_done, w + 1)
                nc.scalar.activation(xi[:, :, TAPS - 1:], bt(psM[:, 0, :]), ACT.Copy).then_inc(s_xi_done, 1)
                act.wait_ge(s_dec_mm, w + 1)
                if w > 0:
                    act.wait_ge(s_ac_done, w)
                nc.scalar.activation(A[:, :], psM[:, 1, :], ACT.Copy, scale=pc("wbase")).then_inc(s_a_raw, 1)
                act.wait_ge(s_dm_done, w + 1)
                if w > 0:
                    act.wait_ge(s_n_done, w)
                nc.scalar.activation(EE[:, :, 1:], dm[:, :, 1:], ACT.Exp).then_inc(s_ee_done, 1)
                act.wait_ge(s_gd_done, w + 1)
                nc.scalar.activation(ge[:, :], gd[:, :], ACT.Exp).then_inc(s_ge_done, 1)
                act.wait_ge(s_so_done, w + 1)
                if 2 * w > 0:
                    act.wait_ge(s_no_done, 2 * w)
                nc.scalar.activation(sde[:, :, :], so[:, :, :], ACT.Exp).then_inc(s_sde_done, 1)
                act.wait_ge(s_t8_done, w + 1)
                nc.scalar.activation(f8[:, :, :], t8[:, :, :], ACT.Exp).then_inc(s_f8_done, 1)
                if w == 0:
                    act.wait_ge(s_wcT_mm, 1)
                    nc.scalar.activation(wcT[:, :, :], psM[:, 1, :].rearrange("p (t n) -> p t n", t=HT), ACT.Copy).then_inc(s_wcT_done, 1)
                ln(ln_of(2, w))
                if w == 0:
                    act.wait_ge(s_ub_done, 2)
                for k in range(HT):
                    act.wait_ge(s_u_mm, HT * w + k + 1)
                    if w > 0:
                        act.wait_ge(s_ffn_mm, w)
                    nc.scalar.activation(u[:, k, :], psF[k % 2][:, :], ACT.Gelu, bias=ubias[:, k:k + 1]).then_inc(s_u_done, 1)
                act.wait_ge(s_ffn_mm, w + 1)
                act.wait_ge(s_x3_done, w + 1)
                nc.scalar.activation(br[:, :], psS[0][:, :], ACT.Identity, bias=dbias[:, 0:1]).then_inc(s_ffn_read, 1)

            act.wait_ge(s_mod_in, 32)
            nc.scalar.activation(csil[:, :, :], csil[:, :, :], ACT.Silu).then_inc(s_csil_done, 1)
            act.wait_ge(s_eps_set, 1)
            for w in range(WINDOWS):
                ln(ln_front(w))
            act.wait_ge(s_col_in, 16)
            pre(0)
            for c in range(2, NCH):
                decays(0, c)
            for w in range(WINDOWS):
                router(w)
                if w + 1 < WINDOWS:
                    pre(w + 1)
                experts(w)
                ssd(w)

        @block.vector
        def _(dve):
            v = nc.vector

            def ln(n, out=None):
                dve.wait_ge(s_ln_sd, n + 1)
                v.reciprocal(rs[:, :], rs[:, :]).then_inc(s_ln_rs, 1)
                dve.wait_ge(s_ln_rs, n + 1)
                out = bt(h2[:, :]) if out is None else out
                v.tensor_tensor(out, bt(psA[:, :]), bt(rs[:, :]), ALU.mult).then_inc(s_ln_n1, 1)

            def modulation():
                dve.wait_ge(s_mod_mm, 1)
                v.tensor_copy(mod[:, :, :], psM[:, 0, 0:12 * NB].rearrange("p (i b) -> p i b", b=NB)).then_inc(s_mod_read, 1)
                dve.wait_ge(s_mod_read, 1)
                scale = mod[:, 1:12:3, :]
                gates = mod[:, 2:12:3, :]
                v.tensor_scalar(scale, scale, 1.0, None, ALU.add).then_inc(s_mod_scale, 1)
                v.tensor_scalar(gsg[:, :, :], gates, 0.0, 2.0, ALU.is_ge, ALU.mult).then_inc(s_mod_sign, 1)
                v.tensor_scalar(gab[:, :, :], gates, -1.0, None, ALU.mult).then_inc(s_mod_neg, 1)
                dve.wait_ge(s_mod_neg, 1)
                v.tensor_tensor(gab[:, :, :], gab[:, :, :], gates, ALU.max).then_inc(s_mod_abs, 1)
                dve.wait_ge(s_mod_sign, 1)
                v.tensor_scalar(gsg[:, :, :], gsg[:, :, :], -1.0, None, ALU.add).then_inc(s_mod_sign, 1)
                dve.wait_ge(s_mod_abs, 1)
                v.tensor_scalar(gab[:, :, :], gab[:, :, :], 0.25, None, ALU.max).then_inc(s_mod_abs, 1)
                dve.wait_ge(s_mod_sign, 2)
                dve.wait_ge(s_mod_abs, 2)
                v.tensor_tensor(gates, gsg[:, :, :], gab[:, :, :], ALU.mult).then_inc(s_mod_done, 1)

            def bias_fold():
                dve.wait_ge(s_fold_in, 48)
                for s in range(STAGES):
                    dve.wait_ge(s_coef_in[s % 2], 16 * (s // 2 + 1))
                    if s > 0:
                        dve.wait_ge(s_bfold_sum, s)
                    pr = bx[:, :].rearrange("p (n h s) -> p n h s", h=2, s=1 << s)
                    d = fb[:, 1, :].rearrange("p (n h s) -> p n h s", h=2, s=1 << s)
                    o = coef[s % 2][0:1, 1, :].rearrange("p (n h s) -> p n h s", h=2, s=1 << s)
                    v.tensor_tensor(fb[:, 0, :], bx[:, :], coef[s % 2][0:1, 0, :], ALU.mult).then_inc(s_bfold_diag, 1)
                    for h in range(2):
                        v.tensor_tensor(d[:, :, h, :], pr[:, :, 1 - h, :], o[:, :, h, :], ALU.mult).then_inc(s_bfold_off, 1)
                    dve.wait_ge(s_bfold_off, 2 * (s + 1))
                    dve.wait_ge(s_bfold_diag, s + 1)
                    v.tensor_tensor(bx[:, :], fb[:, 0, :], fb[:, 1, :], ALU.add).then_inc(s_bfold_sum, 1)

            def pre(w):
                if w > 0:
                    v.tensor_copy(p[:, :, :, 0:HALO], p[:, :, :, TW:TW + HALO]).then_inc(s_carry_done, 1)
                    if w + 1 == WINDOWS:
                        dve.wait_ge(s_carry_done, w + 1)
                        v.memset(p[:, :, :, TW + HALO - 1:], 0.0).then_inc(s_pad_set, 1)
                        dve.wait_ge(s_pad_set, 1)
                dve.wait_ge(s_carry_done, w + 1)
                dve.wait_ge(s_p_done, 3 * (w + 1) + 1)
                if w > 0:
                    dve.wait_ge(s_acc0_mm, w)
                for j in range(TAPS):
                    for i, name in enumerate(["cq", "ck", "cv"]):
                        src = p[:, i, :, j:j + TW]
                        if j == 0:
                            v.tensor_scalar(bt(y[:, i, :]), src, pc(name, j), None, ALU.mult).then_inc(s_conv_tap, 1)
                        else:
                            dve.wait_ge(s_conv_tap, 3 * (TAPS * w + j - 1) + i + 1)
                            v.scalar_tensor_tensor(bt(y[:, i, :]), src, pc(name, j), bt(y[:, i, :]), ALU.mult,
                                                   ALU.add).then_inc(s_conv_tap, 1)
                dve.wait_ge(s_l2_root, w + 1)
                v.tensor_scalar(nrm[:, :, :], nrm[:, :, :], 1.0e-6, None, ALU.add).then_inc(s_l2_eps, 1)
                dve.wait_ge(s_l2_eps, w + 1)
                v.reciprocal(nrm[:, :, :], nrm[:, :, :]).then_inc(s_l2_rn, 1)
                n = 0
                for g, js in enumerate(PACK):
                    dve.wait_ge(s_kk_mm, 4 * w + g + 1)
                    at = 0
                    for j in js:
                        n += 1
                        k = CH - 1 - j
                        dve.wait_ge(s_g_done, 7 * w + CH - 1 - j)
                        dve.wait_ge(s_cp_done, w + 1)
                        v.tensor_tensor(Mj[j][:, :, :], psM[:, g % 2, at:at + BC * k].rearrange("p (g i) -> p g i", i=k),
                                        G[j][:, :, 1:], ALU.mult).then_inc(s_mj_done, 1)
                        at += BC * k
                dve.wait_ge(s_xk_init, w + 1)
                dve.wait_ge(s_mj_done, 7 * (w + 1))
                X = bci(XK[:, :])
                for j in range(CH - 1):
                    k = CH - 1 - j
                    if 7 * w + j > 0:
                        dve.wait_ge(s_xk_sub, 7 * w + j)
                    tmp = tk[:, 0:BC * k].rearrange("p (g i) -> p g i", i=k)
                    v.tensor_tensor(tmp, Mj[j][:, :, :], X[:, :, j:j + 1].broadcast_to([P, BC, k]), ALU.mult).then_inc(s_xk_prod, 1)
                    dve.wait_ge(s_xk_prod, 7 * w + j + 1)
                    v.tensor_tensor(X[:, :, j + 1:], X[:, :, j + 1:], tmp, ALU.subtract).then_inc(s_xk_sub, 1)

            def scan(w):
                dve.wait_ge(s_krep_in, 16 * DH * (w + 1))
                dve.wait_ge(s_wrep_in, 16 * DH * (w + 1))
                dve.wait_ge(s_xv_sub, 7 * (w + 1))
                for c in range(NCH):
                    g = NCH * w + c
                    t0, t1 = c * CH, (c + 1) * CH
                    prev = H[(g - 1) % NH_][:, :, CH].rearrange("p (b e) -> p b e", b=NB)
                    wv = wrep[:, :, :].rearrange("p e (b t) -> p b e t", b=NB)[:, :, :, t0:t1]
                    kv = krep[:, :, :].rearrange("p e (b t) -> p b e t", b=NB)[:, :, :, t0:t1]
                    if g > 0:
                        dve.wait_ge(s_scan_done, g)
                    v.tensor_tensor(Pb[:, :, :, :], wv, prev.unsqueeze(3).broadcast_to([P, NB, DH, CH]), ALU.mult).then_inc(s_prod_done, 1)
                    v.tensor_copy(D1[:, :, 0], H[(g - 1) % NH_][:, :, CH]).then_inc(s_seed_done, 1)
                    dve.wait_ge(s_prod_done, g + 1)
                    v.tensor_reduce(R[:, :, :], Pb[:, :, :, :].rearrange("p b e i -> p b i e"), AX.X, ALU.add).then_inc(s_red_done, 1)
                    dve.wait_ge(s_red_done, g + 1)
                    v.tensor_tensor(U[:, :, :], bt(XV[:, :])[:, :, t0:t1], R[:, :, :], ALU.subtract).then_inc(s_u_delta, 1)
                    dve.wait_ge(s_u_delta, g + 1)
                    v.tensor_tensor(D1[:, :, 1:].rearrange("p (b e) i -> p b e i", b=NB), kv,
                                    U[:, :, :].unsqueeze(2).broadcast_to([P, NB, DH, CH]), ALU.mult).then_inc(s_outer_done, 1)
                    dve.wait_ge(s_outer_done, g + 1)
                    dve.wait_ge(s_seed_done, g + 1)
                    dve.wait_ge(s_a9_done, g + 1)
                    if g - NH_ + 1 > 0:
                        dve.wait_ge(s_qs_done, g - NH_ + 1)
                    v.tensor_tensor_scan(H[g % NH_][:, :, :].rearrange("p s i -> p (s i)"),
                                         A9[g % 2][:, :, :].rearrange("p s i -> p (s i)"),
                                         D1[:, :, :].rearrange("p s i -> p (s i)"), 0.0, ALU.mult,
                                         ALU.add).then_inc(s_scan_done, 1)

            def route(w):
                if HT * w > 0:
                    dve.wait_ge(s_u_mm, HT * w)
                ln(ln_of(0, w))
                dve.wait_ge(s_lg_mm, w + 1)
                if 2 * w > 0:
                    dve.wait_ge(s_route_q, 2 * w)
                v.tensor_tensor(lg[:, :, :], psM[:, 0, 0:TT * EXPERTS].rearrange("p (t e) -> p t e", e=EXPERTS),
                                rb2s[:, :].unsqueeze(1).broadcast_to([P, TT, EXPERTS]), ALU.add).then_inc(s_lg_done, 1)
                dve.wait_ge(s_lg_done, w + 1)
                v.tensor_reduce(lmax[:, :], lg[:, :, :], AX.X, ALU.max).then_inc(s_lmax_done, 1)
                dve.wait_ge(s_lmax_done, w + 1)
                v.tensor_tensor(ls[:, :, :], lg[:, :, :], lmax[:, :].unsqueeze(2).broadcast_to([P, TT, EXPERTS]), ALU.subtract).then_inc(s_ls_done, 1)
                for t in range(TT):
                    mine = lg[:, t, :].unsqueeze(2).broadcast_to([P, EXPERTS, EXPERTS])
                    other = lg[:, t, :].unsqueeze(1).broadcast_to([P, EXPERTS, EXPERTS])
                    v.tensor_tensor(gt[:, t, :, :], other, mine, ALU.is_gt).then_inc(s_cmp_done, 1)
                    v.tensor_tensor(eq[:, t, :, :], other, mine, ALU.is_equal).then_inc(s_cmp_done, 1)
                dve.wait_ge(s_cmp_done, 2 * TT * (w + 1))
                v.tensor_tensor(eq[:, :, :, :].rearrange("p t a b -> p t (a b)"), eq[:, :, :, :].rearrange("p t a b -> p t (a b)"),
                                low[:, :, :].rearrange("p a b -> p (a b)").unsqueeze(1).broadcast_to([P, TT, EXPERTS * EXPERTS]),
                                ALU.mult).then_inc(s_route_q, 1)
                dve.wait_ge(s_route_q, 2 * w + 1)
                v.tensor_tensor(gt[:, :, :, :], gt[:, :, :, :], eq[:, :, :, :], ALU.add).then_inc(s_route_q, 1)
                dve.wait_ge(s_route_q, 2 * w + 2)
                v.tensor_reduce(rank[:, :, :], gt[:, :, :, :], AX.X, ALU.add).then_inc(s_rank_done, 1)
                dve.wait_ge(s_rank_done, w + 1)
                dve.wait_ge(s_ex_done, w + 1)
                v.scalar_tensor_tensor(exm[:, :, :], rank[:, :, :], 1.5, ex[:, :, :], ALU.is_lt, ALU.mult).then_inc(s_exm_done, 1)
                dve.wait_ge(s_exm_done, w + 1)
                v.tensor_reduce(den[:, :], exm[:, :, :], AX.X, ALU.add).then_inc(s_den_done, 1)
                dve.wait_ge(s_den_done, w + 1)
                v.reciprocal(rden[:, :], den[:, :]).then_inc(s_rden_done, 1)
                dve.wait_ge(s_rden_done, w + 1)
                if TT * EXPERTS * w > 0:
                    dve.wait_ge(s_cmb_done, TT * EXPERTS * w)
                v.tensor_tensor(gate[:, :, :], exm[:, :, :], rden[:, :].unsqueeze(2).broadcast_to([P, TT, EXPERTS]), ALU.mult).then_inc(s_gate_done, 1)

            def ssd(w):
                dve.wait_ge(s_yT_mm, w + 1)
                v.tensor_tensor(br[:, :], psM[:, 1, :], h2[:, :], ALU.add).then_inc(s_yf_done, 1)
                dve.wait_ge(s_hid_mm, HT * EXPERTS * (w + 1))
                ln(ln_of(1, w))
                if w == 0:
                    v.memset(xi[:, :, 0:TAPS - 1], 0.0).then_inc(s_halo_done, 1)
                else:
                    dve.wait_ge(s_xc_tap, 4 * w)
                    v.tensor_copy(xi[:, :, 0:TAPS - 1], xi[:, :, TW:TW + TAPS - 1]).then_inc(s_halo_done, 1)
                if w + 1 < WINDOWS:
                    dve.wait_ge(s_qs_done, NCH * (w + 2))
                dve.wait_ge(s_a_raw, w + 1)
                v.tensor_tensor_scan(ac[:, :, :].rearrange("p b t -> p (b t)"), segm[:, :, :].rearrange("p b t -> p (b t)"),
                                     A[:, :], 0.0, ALU.mult, ALU.add).then_inc(s_ac_done, 1)
                dve.wait_ge(s_halo_done, w + 1)
                dve.wait_ge(s_xi_done, w + 1)
                v.tensor_scalar(bt(xc[:, :]), xi[:, :, 0:TW], pc("cx", 0), pc("cb"), ALU.mult, ALU.add).then_inc(s_xc_tap, 1)
                dve.wait_ge(s_ac_done, w + 1)
                v.tensor_tensor_scan(rm[:, :, :].rearrange("p b t -> p (b t)"), segb[:, :, :].rearrange("p b t -> p (b t)"),
                                     ac[:, :, :].rearrange("p b t -> p (b t)"), 0.0, ALU.add, ALU.min).then_inc(s_rm_done, 1)
                dve.wait_ge(s_xc_tap, 4 * w + 1)
                v.scalar_tensor_tensor(bt(xc[:, :]), xi[:, :, 1:1 + TW], pc("cx", 1), bt(xc[:, :]), ALU.mult, ALU.add).then_inc(s_xc_tap, 1)
                dve.wait_ge(s_rm_done, w + 1)
                v.tensor_tensor(dm[:, :, 1:], rm[:, :, 1:], rm[:, :, 0:TW - 1], ALU.subtract).then_inc(s_dm_done, 1)
                dve.wait_ge(s_xc_tap, 4 * w + 2)
                v.scalar_tensor_tensor(bt(xc[:, :]), xi[:, :, 2:2 + TW], pc("cx", 2), bt(xc[:, :]), ALU.mult, ALU.add).then_inc(s_xc_tap, 1)
                v.tensor_tensor(gd[:, :], rm[:, :, :].rearrange("p b t -> p (b t)"), ac[:, :, :].rearrange("p b t -> p (b t)"), ALU.subtract).then_inc(s_gd_done, 1)
                dve.wait_ge(s_xc_tap, 4 * w + 3)
                v.scalar_tensor_tensor(bt(xc[:, :]), xi[:, :, 3:3 + TW], pc("cx", 3), bt(xc[:, :]), ALU.mult, ALU.add).then_inc(s_xc_tap, 1)
                v.tensor_reduce(mx[:, :], ac[:, :, :], AX.X, ALU.max).then_inc(s_mx_done, 1)
                dve.wait_ge(s_mx_done, w + 1)
                v.tensor_tensor(so[:, :, :], ac[:, :, :], mx[:, :].unsqueeze(2).broadcast_to([P, NB, TW]), ALU.subtract).then_inc(s_so_done, 1)
                v.tensor_tensor(t8[:, 0, :], Ms[w % 2][:, :], ac[:, :, TW - 1], ALU.add).then_inc(s_t8_a, 1)
                dve.wait_ge(s_t8_a, w + 1)
                v.tensor_scalar(Ms[(w + 1) % 2][:, :], t8[:, 0, :], 0.0, None, ALU.max).then_inc(s_ms_done, 1)
                dve.wait_ge(s_ms_done, w + 1)
                v.tensor_scalar(t8[:, 1, :], Ms[(w + 1) % 2][:, :], -1.0, None, ALU.mult).then_inc(s_t8_n, 1)
                dve.wait_ge(s_t8_n, w + 1)
                v.tensor_tensor(t8[:, 0, :], t8[:, 0, :], t8[:, 1, :], ALU.add).then_inc(s_t8_done, 1)
                dve.wait_ge(s_ge_done, w + 1)
                dve.wait_ge(s_xc_tap, 4 * w + 4)
                v.tensor_tensor(gx[:, :], ge[:, :], xc[:, :], ALU.mult).then_inc(s_gx_done, 1)
                dve.wait_ge(s_ee_done, w + 1)
                v.tensor_tensor_scan(N[:, :, :].rearrange("p b t -> p (b t)"), EE[:, :, :].rearrange("p b t -> p (b t)"),
                                     ge[:, :], 0.0, ALU.mult, ALU.add).then_inc(s_nd_done, 1)
                dve.wait_ge(s_gx_done, w + 1)
                v.tensor_tensor_scan(Y[:, :, :].rearrange("p b t -> p (b t)"), EE[:, :, :].rearrange("p b t -> p (b t)"),
                                     gx[:, :], 0.0, ALU.mult, ALU.add).then_inc(s_n_done, 1)
                dve.wait_ge(s_sde_done, w + 1)
                if w > 0:
                    dve.wait_ge(s_hs_done, w)
                if w > 0:
                    dve.wait_ge(s_out_mm, w)
                v.tensor_tensor(no[:, :, :], sde[:, :, :], Hs[:, 1, :].unsqueeze(2).broadcast_to([P, NB, TW]), ALU.mult).then_inc(s_no_done, 1)
                v.tensor_tensor(yo[:, :, :], sde[:, :, :], Hs[:, 0, :].unsqueeze(2).broadcast_to([P, NB, TW]), ALU.mult).then_inc(s_no_done, 1)
                dve.wait_ge(s_nd_done, w + 1)
                dve.wait_ge(s_no_done, 2 * w + 1)
                v.tensor_tensor(no[:, :, :], no[:, :, :], N[:, :, :], ALU.add).then_inc(s_nt_done, 1)
                dve.wait_ge(s_n_done, w + 1)
                dve.wait_ge(s_no_done, 2 * w + 2)
                v.tensor_tensor(yo[:, :, :], yo[:, :, :], Y[:, :, :], ALU.add).then_inc(s_yt_done, 1)
                dve.wait_ge(s_nt_done, w + 1)
                v.reciprocal(no[:, :, :], no[:, :, :]).then_inc(s_rN_done, 1)
                dve.wait_ge(s_rN_done, w + 1)
                dve.wait_ge(s_yt_done, w + 1)
                v.tensor_tensor(yo[:, :, :], yo[:, :, :], no[:, :, :], ALU.mult).then_inc(s_yn_done, 1)
                dve.wait_ge(s_f8_done, w + 1)
                v.tensor_tensor(Hs[:, :, :], Hs[:, :, :], f8[:, 0:1, :].broadcast_to([P, 2, NB]), ALU.mult).then_inc(s_hs_a, 1)
                v.tensor_tensor(Yl[:, 0, :], Y[:, :, TW - 1], f8[:, 1, :], ALU.mult).then_inc(s_hs_a, 1)
                v.tensor_tensor(Yl[:, 1, :], N[:, :, TW - 1], f8[:, 1, :], ALU.mult).then_inc(s_hs_a, 1)
                dve.wait_ge(s_hs_a, 3 * (w + 1))
                v.tensor_tensor(Hs[:, :, :], Hs[:, :, :], Yl[:, :, :], ALU.add).then_inc(s_hs_done, 1)
                dve.wait_ge(s_out_mm, w + 1)
                v.tensor_tensor(bt(br[:, :]), bt(psM[:, 0, :]), per_b(GA, 1), ALU.mult).then_inc(s_zo_done, 1)
                dve.wait_ge(s_dec_mm, w + 1)
                ln(ln_of(2, w))

            v.memset(eps[:, :], 1.0e-5).then_inc(s_eps_set, 1)
            v.memset(p[:, :, :, 0:HALO - 1], 0.0).then_inc(s_carry_done, 1)
            for i in range(2):
                v.memset(A9[i][:, :, 0], 0.0).then_inc(s_set, 1)
            v.memset(H[NH_ - 1][:, :, CH], 0.0).then_inc(s_set, 1)
            v.memset(segm[:, :, :], 1.0).then_inc(s_set, 1)
            v.memset(segb[:, :, :], 0.0).then_inc(s_set, 1)
            v.memset(EE[:, :, 0], 0.0).then_inc(s_set, 1)
            v.memset(Ms[0][:, :], 0.0).then_inc(s_set, 1)
            v.memset(Hs[:, :, :], 0.0).then_inc(s_set, 1)
            dve.wait_ge(s_set, 8)
            v.memset(segm[:, :, 0], 0.0).then_inc(s_set, 1)
            v.memset(segb[:, :, 0], BIG).then_inc(s_set, 1)
            dve.wait_ge(s_set, 10)
            ln(0, hf[:, :, 0:TW])
            modulation()
            for w in range(1, WINDOWS):
                ln(ln_front(w), hf[:, :, w * TW:(w + 1) * TW])
            dve.wait_ge(s_col_in, 16)
            v.tensor_tensor(dbias[:, :], pc("bcon"), pc("downb"), ALU.add).then_inc(s_ub_done, 1)
            pre(0)
            bias_fold()
            dve.wait_ge(s_ub_mm, 1)
            v.tensor_tensor(ubias[:, :], psM[:, 0, 0:HT], col[:, COL["upb"]:COL["upb"] + HT], ALU.add).then_inc(s_ub_done, 1)
            scan(0)
            for w in range(WINDOWS):
                if w == 0:
                    dve.wait_ge(s_exp_in, 16 * 5)
                route(w)
                if w + 1 < WINDOWS:
                    pre(w + 1)
                    scan(w + 1)
                ssd(w)

        @block.gpsimd
        def _(pool):
            g_ = nc.gpsimd

            def ln(n, out, s, c, l):
                pool.wait_ge(s_ln_n1, n + 1)
                g_.tensor_tensor(out, out, per_b(c, l), ALU.mult).then_inc(s_ln_n2, 1)
                pool.wait_ge(s_ln_n2, n + 1)
                g_.tensor_tensor(out, out, per_b(s, l), ALU.add).then_inc(s_ln_h, 1)

            def pre(w):
                a = bci(ag[:, :])
                if 7 * w > 0:
                    pool.wait_ge(s_xk_prod, 7 * w)
                pool.wait_ge(s_gates_done, 2 * (w + 1))
                if 16 * w > 0:
                    pool.wait_ge(s_xk_out, 16 * w)
                for j in reversed(range(CH - 1)):
                    n = 7 * w + CH - 2 - j
                    if n > 0:
                        pool.wait_ge(s_g_done, n)
                    g_.tensor_tensor(G[j][:, :, 1:], G[j + 1][:, :, :], a[:, :, j + 1:j + 2].broadcast_to([P, BC, CH - 1 - j]),
                                     ALU.mult).then_inc(s_g_done, 1)
                pool.wait_ge(s_g_done, 7 * (w + 1))
                g_.tensor_tensor(bci(cpd[:, :]), G[0][:, :, :], a[:, :, 0:1].broadcast_to([P, BC, CH]), ALU.mult).then_inc(s_cp_done, 1)
                pool.wait_ge(s_c3_done, w + 1)
                if NCH * w > 0:
                    pool.wait_ge(s_u_delta, NCH * w)
                g_.tensor_tensor(XV[:, :], c3[:, 2, :], bg[:, :], ALU.mult).then_inc(s_vb_done0, 1)
                pool.wait_ge(s_l2_rn, w + 1)
                if 16 * w > 0:
                    pool.wait_ge(s_kn_out, 16 * w)
                g_.tensor_tensor(kn[:, :], c3[:, 1, :], nrm[:, 1, :], ALU.mult).then_inc(s_kn_done, 1)
                if NCH * w > 0:
                    pool.wait_ge(s_qs_done, NCH * w)
                g_.tensor_tensor(qn[:, :], c3[:, 0, :], nrm[:, 0, :], ALU.mult).then_inc(s_qn_done, 1)
                pool.wait_ge(s_kn_done, w + 1)
                g_.tensor_tensor(kb[:, :], kn[:, :], bg[:, :], ALU.mult).then_inc(s_kb_done, 1)
                pool.wait_ge(s_kb_done, w + 1)
                pool.wait_ge(s_qn_done, w + 1)
                k3, b3 = bci(kn[:, :]), bci(kb[:, :])
                for g, js in enumerate(PACK):
                    at = 0
                    for j in js:
                        k = CH - 1 - j
                        g_.tensor_tensor(KK[:, g, at:at + BC * k].rearrange("p (g i) -> p g i", i=k), b3[:, :, j + 1:],
                                         k3[:, :, j:j + 1].broadcast_to([P, BC, k]), ALU.mult).then_inc(s_kk_done, 1)
                        at += BC * k
                if 16 * w > 0:
                    pool.wait_ge(s_xk_out, 16 * w)
                pool.wait_ge(s_cp_done, w + 1)
                g_.tensor_tensor(XK[:, :], kb[:, :], cpd[:, :], ALU.mult).then_inc(s_xk_init, 1)
                pool.wait_ge(s_mj_done, 7 * (w + 1))
                pool.wait_ge(s_vb_done0, w + 1)
                X = bci(XV[:, :])
                for j in range(CH - 1):
                    k = CH - 1 - j
                    if 7 * w + j > 0:
                        pool.wait_ge(s_xv_sub, 7 * w + j)
                    tmp = tv[:, 0:BC * k].rearrange("p (g i) -> p g i", i=k)
                    g_.tensor_tensor(tmp, Mj[j][:, :, :], X[:, :, j:j + 1].broadcast_to([P, BC, k]), ALU.mult).then_inc(s_xv_prod, 1)
                    pool.wait_ge(s_xv_prod, 7 * w + j + 1)
                    g_.tensor_tensor(X[:, :, j + 1:], X[:, :, j + 1:], tmp, ALU.subtract).then_inc(s_xv_sub, 1)

            def read_state(w, c):
                g = NCH * w + c
                pool.wait_ge(s_scan_done, g + 1)
                pool.wait_ge(s_qn_done, w + 1)
                if w > 0:
                    pool.wait_ge(s_attn_mm, w)
                q = bt(qn[:, :])[:, :, c * CH:(c + 1) * CH].unsqueeze(2).broadcast_to([P, NB, DH, CH])
                o = QS[:, :, :].rearrange("p e (b t) -> p b e t", b=NB)[:, :, :, c * CH:(c + 1) * CH]
                g_.tensor_tensor(o, H[g % NH_][:, :, 1:].rearrange("p (b e) i -> p b e i", b=NB), q, ALU.mult).then_inc(s_qs_done, 1)

            def fold(s):
                w_ = wx if s < STAGES else wc
                st = s if s < STAGES else 2 * STAGES - 1 - s
                pool.wait_ge(s_fold_in, 48)
                pool.wait_ge(s_coef_in[s % 2], 16 * (s // 2 + 1))
                if s > 0:
                    pool.wait_ge(s_fold_sum, s)
                v4 = w_[:, :].rearrange("p (n h s) -> p n h s", h=2, s=1 << st)
                d4 = ft[:, 1, :].rearrange("p (n h s) -> p n h s", h=2, s=1 << st)
                o4 = coef[s % 2][:, 1, :].rearrange("p (n h s) -> p n h s", h=2, s=1 << st)
                g_.tensor_tensor(ft[:, 0, :], w_[:, :], coef[s % 2][:, 0, :], ALU.mult).then_inc(s_fold_diag, 1)
                for h in range(2):
                    g_.tensor_tensor(d4[:, :, h, :], v4[:, :, 1 - h, :], o4[:, :, h, :], ALU.mult).then_inc(s_fold_off, 1)
                pool.wait_ge(s_fold_diag, s + 1)
                pool.wait_ge(s_fold_off, 2 * (s + 1))
                g_.tensor_tensor(w_[:, :], ft[:, 0, :], ft[:, 1, :], ALU.add).then_inc(s_fold_sum, 1)

            def add_expert(w, e):
                n = EXPERTS * w + e
                pool.wait_ge(s_cmb_done, TT * (n + 1))
                pool.wait_ge(s_acc0_done, w + 1)
                if n > 0:
                    pool.wait_ge(s_acc_done, n)
                g_.tensor_tensor(acc[:, :, :], acc[:, :, :], cmb[n % 2][:, :, :], ALU.add).then_inc(s_acc_done, 1)

            for j in range(CH):
                g_.memset(G[j][:, :, 0], 1.0).then_inc(s_g_set, 1)
            pool.wait_ge(s_g_set, CH)
            pool.wait_ge(s_mod_done, 1)
            pool.wait_ge(s_mod_scale, 1)
            for w in range(WINDOWS):
                ln(ln_front(w), hf[:, :, w * TW:(w + 1) * TW], SA, CA, 0)
            pool.wait_ge(s_gates_done, 2)
            pre(0)
            for s in range(STAGES):
                fold(s)
            for c in range(NCH):
                fold(STAGES + c)
                read_state(0, c)
            fold(2 * STAGES - 1)
            for w in range(WINDOWS):
                pool.wait_ge(s_ao_done, w + 1)
                g_.tensor_tensor(bt(br[:, :]), bt(br[:, :]), per_b(GA, 0), ALU.mult).then_inc(s_aog_done, 1)
                pool.wait_ge(s_aog_done, w + 1)
                g_.tensor_tensor(x[:, w, :], x[:, w, :], br[:, :], ALU.add).then_inc(s_x1_done, 1)
                ln(ln_of(0, w), bt(h2[:, :]), SB, CB, 0)
                if w + 1 < WINDOWS:
                    pre(w + 1)
                for e in range(EXPERTS):
                    add_expert(w, e)
                    if w + 1 < WINDOWS:
                        read_state(w + 1, e)
                pool.wait_ge(s_yf_done, w + 1)
                g_.tensor_tensor(bt(br[:, :]), bt(br[:, :]), per_b(GB, 0), ALU.mult).then_inc(s_yg_done, 1)
                pool.wait_ge(s_yg_done, w + 1)
                g_.tensor_tensor(x[:, w, :], x[:, w, :], br[:, :], ALU.add).then_inc(s_x2_done, 1)
                ln(ln_of(1, w), bt(h3[:, :]), SA, CA, 1)
                pool.wait_ge(s_zo_done, w + 1)
                g_.tensor_tensor(x[:, w, :], x[:, w, :], br[:, :], ALU.add).then_inc(s_x3_done, 1)
                ln(ln_of(2, w), bt(h4[:, :]), SB, CB, 1)
                pool.wait_ge(s_ffn_read, w + 1)
                g_.tensor_tensor(bt(br[:, :]), bt(br[:, :]), per_b(GB, 1), ALU.mult).then_inc(s_y4_done, 1)
                pool.wait_ge(s_y4_done, w + 1)
                g_.tensor_tensor(x[:, w, :], x[:, w, :], br[:, :], ALU.add).then_inc(s_x4_done, 1)


def kernel(**inputs):
    import concourse.bacc as bacc
    from concourse.bass_utils import run_bass_kernel_spmd as run

    a = {k: np.asarray(v) for k, v in inputs.items()}
    f32 = np.float32

    xT = a["L0_attn_x"].reshape(NB, WINDOWS, TW, P).transpose(3, 1, 0, 2).reshape(P, WINDOWS, COLS)
    rep = lambda v, axis=0: np.repeat(v, DH, axis=axis)
    win = a["L1_attn_in_proj_w"]
    mats = np.stack([a["L0_attn_Wq"].T, a["L0_attn_Wk"].T, a["L0_attn_Wv"].T, rep(a["L0_attn_Wa"]).T,
                     rep(a["L0_attn_Wb"]).T, a["L0_ffn_rw1"], win[:P].T, rep(win[P:]).T, a["L1_attn_out_proj_w"].T], axis=1)
    head = np.arange(P) // DH
    eye = np.eye(P, dtype=f32)
    consts = np.stack([eye - f32(1.0 / P), np.full((P, P), 1.0 / P, f32),
                       (head[:, None] == head[None, :]).astype(f32), eye], axis=1)
    cols = np.concatenate([
        a["L0_attn_bq"][:, None], a["L0_attn_bk"][:, None], a["L0_attn_bv"][:, None],
        rep(a["L0_attn_ba"])[:, None], rep(a["L0_attn_bb"])[:, None], a["L0_attn_bo"][:, None], a["L0_ffn_rb1"][:, None],
        a["L0_attn_conv_q"][:, 0], a["L0_attn_conv_k"][:, 0], a["L0_attn_conv_v"][:, 0], a["L1_attn_conv_w"][:, 0],
        a["L1_attn_conv_b"][:, None], rep(a["L1_attn_w_base"])[:, None],
        a["L0_ffn_be1"].reshape(EXPERTS * HT, P).T, a["L1_ffn_up_bias"].reshape(HT, P).T,
        a["L1_ffn_b_con"][:, None], a["L1_ffn_down_bias"][:, None]], axis=1)
    cT = np.stack([a["L0_c"].T, a["L1_c"].T], axis=1)
    wmod = np.stack([a["L0_wmod"], a["L1_wmod"]], axis=1)
    wo_rep = rep(a["L0_attn_Wo"].T.reshape(HEADS, DH, P))
    we1 = a["L0_ffn_we1"].transpose(1, 0, 2)
    we2 = a["L0_ffn_we2"].reshape(EXPERTS, HT, P, P).transpose(2, 0, 1, 3)
    lower = np.tril(np.ones((EXPERTS, EXPERTS), f32), -1)

    def coefficients(wts, transposed):
        out = []
        order = range(STAGES)
        for s in (reversed(order) if transposed else order):
            q = wts[s].reshape(-1, 1 << s, 2, 2)
            same = np.stack([q[:, :, 0, 0], q[:, :, 1, 1]], axis=1)
            cross = [q[:, :, 0, 1], q[:, :, 1, 0]]
            cross = np.stack(cross[::-1] if transposed else cross, axis=1)
            out.append(np.stack([same.reshape(-1), cross.reshape(-1)]))
        return np.stack(out)

    arrays = {
        "xT": xT, "mats": mats, "consts": consts, "cols": cols, "cT": cT, "wmod": wmod, "wo_rep": wo_rep,
        "rw2": a["L0_ffn_rw2"], "rb2": a["L0_ffn_rb2"], "be2": a["L0_ffn_be2"], "we1": we1, "we2": we2,
        "lower": lower, "w_exp": a["L1_ffn_W_exp"], "b_exp": a["L1_ffn_b_exp"][None, :], "w_conT": a["L1_ffn_W_con"].T,
        "up_coef": coefficients(a["L1_ffn_up_weights"], False), "down_coef": coefficients(a["L1_ffn_down_weights"], True),
    }
    nc = bacc.Bacc("TRN2", target_bir_lowering=False, num_devices=1)
    feed, aps = {}, []
    for name, v in arrays.items():
        v = np.ascontiguousarray(v)
        feed[name + "_dram"] = v
        aps.append(nc.dram_tensor(name + "_dram", v.shape, mybir.dt.from_np(v.dtype), kind="ExternalInput").ap())
    aps.append(nc.dram_tensor("scratch_dram", [WINDOWS, 2, P, COLS], fp32, kind="Internal").ap())
    aps.append(nc.dram_tensor("outT_dram", [P, WINDOWS, COLS], fp32, kind="ExternalOutput").ap())
    program(nc, *aps)
    r = run(nc, [feed], core_ids=[0])
    got = r.results[0]["outT_dram"].reshape(P, WINDOWS, NB, TW)
    return np.ascontiguousarray(got.transpose(2, 1, 3, 0).reshape(NB, SEQ, P))
```

```python
from contextlib import ExitStack

import numpy as np
import concourse.bass as bass
from concourse import mybir
from concourse.alu_op_type import AluOpType as ALU

P = 128
NB, SEQ = 8, 256
HEADS, DH = 16, 8
WINDOWS = 4
TW = SEQ // WINDOWS
COLS = NB * TW
CH = 8
NCH = TW // CH
BC = NB * NCH
TAPS = 4
EXPERTS, HID = 8, 512
HT = HID // P
TT = COLS // P
STAGES = 9
BIG = 1.0e30
fp32 = mybir.dt.float32
ACT = mybir.ActivationFunctionType
AX = mybir.AxisListType

_w = [("bq", 1), ("bk", 1), ("bv", 1), ("ba", 1), ("bb", 1), ("bo", 1), ("rb1", 1),
      ("cq", TAPS), ("ck", TAPS), ("cv", TAPS), ("cx", TAPS), ("cb", 1), ("wbase", 1),
      ("be1", EXPERTS * HT), ("upb", HT), ("bcon", 1), ("downb", 1)]
COL, _n = {}, 0
for _name, _k in _w:
    COL[_name] = _n
    _n += _k
NCOL = _n
MATS = ["wq", "wk", "wv", "wa", "wb", "rw1", "win", "wdec", "wout"]
CONSTS = ["center", "mean", "headones", "ident"]
SA, CA, GA, SB, CB, GB = range(6)
PACK = [(0, 6), (1, 5), (2, 4), (3,)]


def program(nc, xT, mats, consts, cols, cT, wmod, wo_rep, rw2, rb2, be2, we1, we2, lower, w_exp, b_exp,
            w_conT, up_coef, down_coef, scratch, outT):
    ctx = ExitStack()
    with ctx:
        def sb(name, *shape):
            return ctx.enter_context(nc.sbuf_tensor(name, list(shape), fp32))

        def sem(name):
            return ctx.enter_context(nc.semaphore(name))

        x = sb("x", P, WINDOWS, COLS)
        M = sb("M", P, len(MATS), P)
        C = sb("C", P, len(CONSTS), P)
        col = sb("col", P, NCOL)
        csil = sb("csil", P, 2, NB)
        eps = sb("eps", P, 2)
        mod = sb("mod", P, 12, NB)
        gsg = sb("gsg", P, 4, NB)
        gab = sb("gab", P, 4, NB)
        worep = sb("worep", P, DH, P)
        rw2s = sb("rw2s", P, EXPERTS)
        rb2s = sb("rb2s", P, EXPERTS)
        be2s = sb("be2s", EXPERTS, P)
        we1s = sb("we1s", P, EXPERTS, HID)
        we2s = sb("we2s", P, EXPERTS, HT, P)
        low = sb("low", P, EXPERTS, EXPERTS)
        sq = sb("sq", P, COLS)
        rs = sq
        hf = sb("hf", P, NB, SEQ)
        h2 = sb("h2", P, COLS)
        hS = sb("hS", P, COLS)
        HALO = TAPS - 1
        p = sb("p", P, 3, NB, TW + HALO)
        ag = sb("ag", P, COLS)
        bg = sb("bg", P, COLS)
        G = [sb(f"G{j}", P, BC, CH - j) for j in range(CH)]
        Mj = [G[j][:, :, 1:] for j in range(CH - 1)]
        XK = sb("XK", P, COLS)
        cpd = XK
        krep = sb("krep", P, DH, COLS)
        wrep = sb("wrep", P, DH, COLS)
        wm = wrep[:, 0:3, :].rearrange("p a n -> p (a n)").rearrange("p (l n) -> p l n", l=2)
        A9 = [sb(f"A9{i}", P, NB * DH, CH + 1) for i in range(2)]
        R = sb("R", P, NB, CH)
        U = sb("U", P, NB, CH)
        D1 = sb("D1", P, NB * DH, CH + 1)
        NH_ = 3
        H = [sb(f"H{i}", P, NB * DH, CH + 1) for i in range(NH_)]
        br = sb("br", P, COLS)
        brS = sb("brS", P, COLS)

        work = sb("work", P, 3 + DH, COLS)
        c3 = y = work[:, 0:3, :]
        qn, kn, XV = (work[:, i, :] for i in range(3))
        QS = work[:, 3:, :]
        KK = work[:, 3:7, :]
        sq2 = work[:, 3:5, :]
        nrm = work[:, 5:7, :]
        kb = work[:, 7, :]
        tk = work[:, 8, :]
        tv = work[:, 9, :]
        pbuf = sb("pbuf", P, COLS)
        Pb = pbuf[:, :].rearrange("p (b e i) -> p b e i", b=NB, e=DH)
        r1 = pbuf
        gateT = pbuf[0:EXPERTS, :].rearrange("p (t n) -> p t n", t=TT)
        ssdb = sb("ssdb", P, 4, COLS)
        xc, A, ge = ssdb[:, 0, :], ssdb[:, 1, :], ssdb[:, 2, :]
        gd, gx = ge, xc

        def timed(i):
            return ssdb[:, i, :].rearrange("p (b t) -> p b t", b=NB)
        Y, ac, N, rm = timed(0), timed(1), timed(2), timed(3)
        so = sde = no = ac
        yo = rm
        lg = sb("lg", P, TT, EXPERTS)
        rank = sb("rank", P, TT, EXPERTS)
        lmax = sb("lmax", P, TT)
        ls = sb("ls", P, TT, EXPERTS)
        ex = ls
        exm = sb("exm", P, TT, EXPERTS)
        den = sb("den", P, TT)
        rden = sb("rden", P, TT)
        gate = sb("gate", P, TT, EXPERTS)
        hidb = sb("hid", P, 2 * HT, COLS)
        hid = [hidb[:, i * HT:(i + 1) * HT, :] for i in range(2)]
        cmbb = sb("cmb", P, 2, COLS)
        cmb = [cmbb[:, i, :].rearrange("p (t n) -> p t n", t=TT) for i in range(2)]
        acc = sb("acc", P, TT, P)
        gt = cmbb[:, 0, 0:TT * EXPERTS * EXPERTS].rearrange("p (t a b) -> p t a b", t=TT, a=EXPERTS)
        eq = cmbb[:, 0, TT * EXPERTS * EXPERTS:].rearrange("p (t a b) -> p t a b", t=TT, a=EXPERTS)
        xi = sb("xi", P, NB, TW + HALO)
        segm = sb("segm", P, NB, TW)
        segb = sb("segb", P, NB, TW)
        EE = sb("EE", P, NB, TW)
        dm = EE
        mx = sb("mx", P, NB)
        Ms = [sb(f"Ms{i}", P, NB) for i in range(2)]
        t8 = sb("t8", P, 2, NB)
        f8 = sb("f8", P, 2, NB)
        Hs = sb("Hs", P, 2, NB)
        Yl = sb("Yl", P, 2, NB)
        wx = sb("wx", P, HID)
        wc = sb("wc", P, HID)
        coef = [hidb[:, 2 * i:2 * i + 2, :] for i in range(2)]
        ft = hidb[:, 4:6, :]
        bx = hidb[0:1, 6, :]
        fb = cmbb[0:1, :, :]
        ubias = sb("ubias", P, HT)
        dbias = sb("dbias", P, 1)
        wcT = wc[:, :].rearrange("p (t n) -> p t n", t=HT)
        u = hidb[:, 0:HT, :]

        s_x0_in = sem("x0_in")
        s_const_in = sem("const_in")
        s_mod_in = sem("mod_in")
        s_col_in = sem("col_in")
        s_mat_in = sem("mat_in")
        s_x_in = sem("x_in")
        s_fold_in = sem("fold_in")
        s_exp_in = sem("exp_in")
        s_we1_in = sem("we1_in")
        s_we2_in = sem("we2_in")
        s_fold_off = sem("fold_off")
        s_bfold_off = sem("bfold_off")
        s_coef_in = [sem(f"coef_in{i}") for i in range(2)]
        s_mod_mm = sem("mod_mm")
        s_kn_done = sem("kn_done")
        s_kn_out = sem("kn_out")
        s_outer_done = sem("outer_done")
        s_krep_in = sem("krep_in")
        s_xk_sub = sem("xk_sub")
        s_xk_out = sem("xk_out")
        s_prod_done = sem("prod_done")
        s_wrep_in = sem("wrep_in")
        s_x4_done = sem("x4_done")
        s_stored = sem("stored")
        s_ln_n1 = sem("ln_n1")
        s_ln_c = sem("ln_c")
        s_ln_sq = sem("ln_sq")
        s_ln_v = sem("ln_v")
        s_csil_done = sem("csil_done")
        s_ln_h = sem("ln_h")
        s_mod_read = sem("mod_read")
        s_proj0_mm = sem("proj0_mm")
        s_hid_done = sem("hid_done")
        s_cmb_done = sem("cmb_done")
        s_yf_done = sem("yf_done")
        s_mj_done = sem("mj_done")
        s_lgT_read = sem("lgT_read")
        s_p_done = sem("p_done")
        s_gates_done = sem("gates_done")
        s_proj_mm = sem("proj_mm")
        s_l2_sq = sem("l2_sq")
        s_l2_mm = sem("l2_mm")
        s_kk_done = sem("kk_done")
        s_l2_root = sem("l2_root")
        s_kk_mm = sem("kk_mm")
        s_qs_done = sem("qs_done")
        s_ub_done = sem("ub_done")
        s_ffn_read = sem("ffn_read")
        s_attn_mm = sem("attn_mm")
        s_r1_mm = sem("r1_mm")
        s_r1_done = sem("r1_done")
        s_ao_done = sem("ao_done")
        s_lg_mm = sem("lg_mm")
        s_gate_done = sem("gate_done")
        s_gT_mm = sem("gT_mm")
        s_acc0_mm = sem("acc0_mm")
        s_hid_mm = sem("hid_mm")
        s_eo_mm = sem("eo_mm")
        s_u_done = sem("u_done")
        s_acc_done = sem("acc_done")
        s_yT_mm = sem("yT_mm")
        s_in_mm = sem("in_mm")
        s_dec_mm = sem("dec_mm")
        s_yn_done = sem("yn_done")
        s_xi_done = sem("xi_done")
        s_out_mm = sem("out_mm")
        s_bfold_sum = sem("bfold_sum")
        s_ub_mm = sem("ub_mm")
        s_fold_sum = sem("fold_sum")
        s_wcT_mm = sem("wcT_mm")
        s_zo_done = sem("zo_done")
        s_a_raw = sem("a_raw")
        s_u_mm = sem("u_mm")
        s_wcT_done = sem("wcT_done")
        s_acc0_done = sem("acc0_done")
        s_ffn_mm = sem("ffn_mm")
        s_x2_done = sem("x2_done")
        s_x1_done = sem("x1_done")
        s_x3_done = sem("x3_done")
        s_ln_log = sem("ln_log")
        s_ln_sd = sem("ln_sd")
        s_carry_done = sem("carry_done")
        s_xk_init = sem("xk_init")
        s_conv_tap = sem("conv_tap")
        s_c3_done = sem("c3_done")
        s_l2_log = sem("l2_log")
        s_l2_rn = sem("l2_rn")
        s_scan_done = sem("scan_done")
        s_a9_done = sem("a9_done")
        s_red_done = sem("red_done")
        s_ls_done = sem("ls_done")
        s_ex_done = sem("ex_done")
        s_halo_done = sem("halo_done")
        s_nt_done = sem("nt_done")
        s_dm_done = sem("dm_done")
        s_ee_done = sem("ee_done")
        s_gd_done = sem("gd_done")
        s_ge_done = sem("ge_done")
        s_so_done = sem("so_done")
        s_sde_done = sem("sde_done")
        s_t8_done = sem("t8_done")
        s_f8_done = sem("f8_done")
        s_no_log = sem("no_log")
        s_rN_done = sem("rN_done")
        s_eps_set = sem("eps_set")
        s_set = sem("set")
        s_mod_scale = sem("mod_scale")
        s_mod_sign = sem("mod_sign")
        s_mod_neg = sem("mod_neg")
        s_mod_abs = sem("mod_abs")
        s_mod_done = sem("mod_done")
        s_bfold_diag = sem("bfold_diag")
        s_pad_set = sem("pad_set")
        s_g_done = sem("g_done")
        s_cp_done = sem("cp_done")
        s_xk_prod = sem("xk_prod")
        s_xv_sub = sem("xv_sub")
        s_seed_done = sem("seed_done")
        s_u_delta = sem("u_delta")
        s_route_q = sem("route_q")
        s_lg_done = sem("lg_done")
        s_lmax_done = sem("lmax_done")
        s_cmp_done = sem("cmp_done")
        s_rank_done = sem("rank_done")
        s_exm_done = sem("exm_done")
        s_den_done = sem("den_done")
        s_rden_done = sem("rden_done")
        s_xc_tap = sem("xc_tap")
        s_ac_done = sem("ac_done")
        s_rm_done = sem("rm_done")
        s_t8_a = sem("t8_a")
        s_mx_done = sem("mx_done")
        s_ms_done = sem("ms_done")
        s_t8_n = sem("t8_n")
        s_gx_done = sem("gx_done")
        s_nd_done = sem("nd_done")
        s_n_done = sem("n_done")
        s_hs_done = sem("hs_done")
        s_no_done = sem("no_done")
        s_yt_done = sem("yt_done")
        s_hs_a = sem("hs_a")
        s_ln_n2 = sem("ln_n2")
        s_qn_done = sem("qn_done")
        s_kb_done = sem("kb_done")
        s_vb_done0 = sem("vb_done0")
        s_xv_prod = sem("xv_prod")
        s_fold_diag = sem("fold_diag")
        s_g_set = sem("g_set")
        s_yg_done = sem("yg_done")
        s_aog_done = sem("aog_done")
        s_y4_done = sem("y4_done")

        def pb(name, *shape):
            return ctx.enter_context(nc.psum_tensor(name, list(shape), fp32))
        psA = pb("psA", P, COLS)
        psB = pb("psB", P, COLS)
        psF = [pb(f"psF{i}", P, COLS) for i in range(2)]
        psS = [pb(f"psS{i}", P, COLS) for i in range(2)]
        psM = pb("psM", P, 2, COLS)

        def m(name):
            return M[:, MATS.index(name), :]

        def cst(name):
            return C[:, CONSTS.index(name), :]

        def pc(name, i=0):
            return col[:, COL[name] + i:COL[name] + i + 1]

        def bt(ap):
            return ap.rearrange("p (b t) -> p b t", b=NB)

        def bci(ap):
            return ap.rearrange("p (g i) -> p g i", i=CH)

        def per_b(i, l=0):
            return mod[:, 6 * l + i, :].unsqueeze(2).broadcast_to([P, NB, TW])

        def ln_front(w):
            return w

        def ln_moe(w):
            return WINDOWS if w == 0 else WINDOWS - 1 + 3 * w

        def ln_ssd(v):
            return WINDOWS + 1 + 3 * v

        def ln_ffn(v):
            return ln_ssd(v) + (2 if v + 1 < WINDOWS else 1)

        block = ctx.enter_context(nc.Block())

        @block.sync
        def _(sp):
            sp.dma_start(x[:, 0, :], xT[:, 0, :]).then_inc(s_x0_in, 16)
            sp.dma_start(C[:, :, :], consts).then_inc(s_const_in, 16)
            sp.dma_start(csil[:, :, :], cT).then_inc(s_mod_in, 16)
            sp.dma_start(wm[:, :, :], wmod).then_inc(s_mod_in, 16)
            sp.dma_start(col[:, :], cols).then_inc(s_col_in, 16)
            sp.dma_start(M[:, :, :], mats).then_inc(s_mat_in, 16)
            for w in range(1, WINDOWS):
                sp.dma_start(x[:, w, :], xT[:, w, :]).then_inc(s_x_in, 16)
            sp.dma_start(bx[:, :], b_exp).then_inc(s_fold_in, 16)
            sp.dma_start(wx[:, :], w_exp).then_inc(s_fold_in, 16)
            sp.dma_start(wc[:, :], w_conT).then_inc(s_fold_in, 16)
            sp.dma_start(worep[:, :, :], wo_rep).then_inc(s_exp_in, 16)
            sp.dma_start(rw2s[:, :], rw2).then_inc(s_exp_in, 16)
            sp.dma_start(rb2s[:, :], rb2.partition_broadcast(P)).then_inc(s_exp_in, 16)
            sp.dma_start(be2s[:, :], be2).then_inc(s_exp_in, 16)
            sp.dma_start(low[:, :, :], lower.partition_broadcast(P)).then_inc(s_exp_in, 16)
            sp.dma_start(we1s[:, :, :], we1).then_inc(s_we1_in, 16)
            sp.dma_start(we2s[:, :, :, :], we2).then_inc(s_we2_in, 16)

            def fold_load(s):
                src, i = (up_coef, s) if s < STAGES else (down_coef, s - STAGES)
                if s >= 2:
                    sp.wait_ge(s_fold_off, 2 * (s - 1))
                    sp.wait_ge(s_bfold_off, 2 * min(s - 1, STAGES))
                sp.dma_start(coef[s % 2][:, :, :], src[i].partition_broadcast(P)).then_inc(s_coef_in[s % 2], 16)

            def spread_keys(w):
                sp.wait_ge(s_mod_mm, 1)
                sp.wait_ge(s_kn_done, w + 1)
                sp.dma_start(scratch[w, 0, :, :], kn[:, :]).then_inc(s_kn_out, 16)
                sp.wait_ge(s_kn_out, 16 * (w + 1))
                if NCH * w > 0:
                    sp.wait_ge(s_outer_done, NCH * w)
                for d in range(DH):
                    sp.dma_start(krep[d::DH, :, :], scratch[w, 0, :, :].rearrange("(h e) n -> h e n", e=DH)).then_inc(s_krep_in, 16)

            def spread_solved(w):
                sp.wait_ge(s_xk_sub, (CH - 1) * (w + 1))
                sp.dma_start(scratch[w, 1, :, :], XK[:, :]).then_inc(s_xk_out, 16)
                sp.wait_ge(s_xk_out, 16 * (w + 1))
                if NCH * w > 0:
                    sp.wait_ge(s_prod_done, NCH * w)
                for d in range(DH):
                    sp.dma_start(wrep[d::DH, :, :], scratch[w, 1, :, :].rearrange("(h e) n -> h e n", e=DH)).then_inc(s_wrep_in, 16)

            def store(v):
                sp.wait_ge(s_x4_done, v + 1)
                sp.dma_start(outT[:, v, :], x[:, v, :]).then_inc(s_stored, 16)

            fold_load(0)
            fold_load(1)
            spread_keys(0)
            spread_solved(0)
            for s in range(2, 2 * STAGES):
                fold_load(s)
            for w in range(WINDOWS + 1):
                if w + 1 < WINDOWS:
                    spread_keys(w + 1)
                    spread_solved(w + 1)
                if w > 0:
                    store(w - 1)
            sp.wait_ge(s_stored, 16 * WINDOWS)

        @block.tensor
        def _(pe):
            mm = nc.tensor.matmul

            def ln(n, src):
                if n > 0:
                    pe.wait_ge(s_ln_n1, n)
                mm(psA[:, :], cst("center"), src, start=True, stop=True).then_inc(s_ln_c, 1)
                pe.wait_ge(s_ln_sq, n + 1)
                mm(psB[:, :], cst("mean"), sq[:, :], start=True, stop=True).then_inc(s_ln_v, 1)

            def modulation():
                pe.wait_ge(s_csil_done, 1)
                for l in range(2):
                    for i in range(6):
                        last = mm(psM[:, 0, (6 * l + i) * NB:(6 * l + i + 1) * NB], wm[:, l, i * P:(i + 1) * P],
                                  csil[:, l, :], start=True, stop=True)
                last.then_inc(s_mod_mm, 1)

            def project(n):
                if n == 0:
                    pe.wait_ge(s_ln_h, WINDOWS)
                    pe.wait_ge(s_mod_read, 1)
                    for i, name in enumerate(["wq", "wk", "wv"]):
                        last = mm(psM[:, 0, i * NB:(i + 1) * NB], m(name), hf[:, :, 0:1], start=True, stop=True)
                    last.then_inc(s_proj0_mm, 1)
                else:
                    if HT * EXPERTS * (n - 1) > 0:
                        pe.wait_ge(s_hid_done, HT * EXPERTS * (n - 1))
                    if TT * EXPERTS * (n - 1) > 0:
                        pe.wait_ge(s_cmb_done, TT * EXPERTS * (n - 1))
                    if n - 1 > 0:
                        pe.wait_ge(s_yf_done, n - 1)
                    pe.wait_ge(s_mj_done, 7 * n)
                    if n - 1 > 0:
                        pe.wait_ge(s_lgT_read, n - 1)
                    pe.wait_ge(s_p_done, 4)
                    pe.wait_ge(s_gates_done, 2 * n)
                cols = TW if n + 1 < WINDOWS else TW - 1
                bank = [psF[0], psF[1], psS[0]]
                for i, name in enumerate(["wq", "wk", "wv"]):
                    mm(bank[i][:, 0:NB * cols], m(name), hf[:, :, n * TW + 1:n * TW + 1 + cols], start=True,
                       stop=True).then_inc(s_proj_mm, 1)
                for name, bank in (("wa", psS[1][:, :]), ("wb", psM[:, 1, :])):
                    mm(bank, m(name), hf[:, :, n * TW:(n + 1) * TW], start=True, stop=True).then_inc(s_proj_mm, 1)

            def square_sums(n):
                pe.wait_ge(s_l2_sq, n + 1)
                pe.wait_ge(s_p_done, 3 * n + 4)
                pe.wait_ge(s_gates_done, 2 * (n + 1))
                for i in range(2):
                    mm(psS[i][:, :], cst("mean"), sq2[:, i, :], start=True, stop=True).then_inc(s_l2_mm, 1)

            def key_products(n):
                for g, js in enumerate(PACK):
                    pe.wait_ge(s_kk_done, 7 * n + sum(len(q) for q in PACK[:g + 1]))
                    if g < 2:
                        pe.wait_ge(s_l2_root, 2 * (n + 1))
                    else:
                        pe.wait_ge(s_mj_done, 7 * n + sum(len(q) for q in PACK[:g - 1]))
                    cols = sum((CH - 1 - j) * BC for j in js)
                    mm(psS[g % 2][:, 0:cols], cst("headones"), KK[:, g, 0:cols], start=True, stop=True).then_inc(s_kk_mm, 1)

            def attn_out(w):
                pe.wait_ge(s_qs_done, NCH * (w + 1))
                if w == 0:
                    pe.wait_ge(s_ub_done, 2)
                if w - 1 > 0:
                    pe.wait_ge(s_ffn_read, w - 1)
                for e in range(DH):
                    last = mm(psM[:, 0, :], worep[:, e, :], QS[:, e, :], start=(e == 0), stop=(e == DH - 1))
                last.then_inc(s_attn_mm, 1)

            def router(w):
                pe.wait_ge(s_ln_h, ln_moe(w) + 1)
                pe.wait_ge(s_gates_done, 2 * min(w + 2, WINDOWS))
                if w > 0:
                    pe.wait_ge(s_lgT_read, w)
                mm(psM[:, 1, :], m("rw1"), h2[:, :], start=True, stop=True).then_inc(s_r1_mm, 1)
                pe.wait_ge(s_r1_done, w + 1)
                pe.wait_ge(s_ao_done, w + 1)
                for t in range(TT):
                    last = mm(psM[:, 0, t * EXPERTS:(t + 1) * EXPERTS], r1[:, t * P:(t + 1) * P], rw2s[:, :],
                              start=True, stop=True)
                last.then_inc(s_lg_mm, 1)

            def router_bias(w):
                pe.wait_ge(s_gate_done, w + 1)
                for t in range(TT):
                    last = nc.tensor.transpose(psM[0:EXPERTS, 1, t * P:(t + 1) * P], gate[:, t, :], cst("ident"))
                last.then_inc(s_gT_mm, 1)
                pe.wait_ge(s_lgT_read, w + 1)
                for t in range(TT):
                    last = mm(psM[:, 0, t * P:(t + 1) * P], gateT[:, t, :], be2s[:, :], start=True, stop=True)
                last.then_inc(s_acc0_mm, 1)

            def experts(w):
                def first(e):
                    for k in range(HT):
                        n = HT * (EXPERTS * w + e) + k
                        if n - 1 > 0:
                            pe.wait_ge(s_hid_done, n - 1)
                        mm(psF[n % 2][:, :], we1s[:, e, k * P:(k + 1) * P], h2[:, :], start=True,
                           stop=True).then_inc(s_hid_mm, 1)

                def second(e):
                    n = EXPERTS * w + e
                    pe.wait_ge(s_hid_done, HT * (n + 1))
                    if TT * (n - 1) > 0:
                        pe.wait_ge(s_cmb_done, TT * (n - 1))
                    for t in range(TT):
                        for k in range(HT):
                            last = mm(psS[n % 2][:, t * P:(t + 1) * P], hid[n % 2][:, k, t * P:(t + 1) * P],
                                      we2s[:, e, k, :], start=(k == 0), stop=(k == HT - 1))
                    last.then_inc(s_eo_mm, 1)

                pe.wait_ge(s_p_done, 1 + 3 * min(w + 2, WINDOWS))
                pe.wait_ge(s_mj_done, 7 * min(w + 2, WINDOWS))
                if HT * w > 0:
                    pe.wait_ge(s_u_done, HT * w)
                if w > 0:
                    pe.wait_ge(s_yf_done, w)
                first(0)
                for e in range(1, EXPERTS):
                    first(e)
                    second(e - 1)
                second(EXPERTS - 1)

            def experts_back(v):
                pe.wait_ge(s_acc_done, EXPERTS * (v + 1))
                for t in range(TT):
                    last = nc.tensor.transpose(psS[0][:, t * P:(t + 1) * P], acc[:, t, :], cst("ident"))
                last.then_inc(s_yT_mm, 1)

            def ssd_in(v):
                pe.wait_ge(s_ln_h, ln_ssd(v) + 1)
                pe.wait_ge(s_p_done, 1 + 3 * min(v + 3, WINDOWS))
                pe.wait_ge(s_hid_done, HT * EXPERTS * (v + 1))
                mm(psF[0][:, :], m("win"), hS[:, :], start=True, stop=True).then_inc(s_in_mm, 1)
                mm(psF[1][:, :], m("wdec"), hS[:, :], start=True, stop=True).then_inc(s_dec_mm, 1)

            def ssd_out(v):
                pe.wait_ge(s_yn_done, v + 1)
                pe.wait_ge(s_xi_done, v + 1)
                mm(psF[0][:, :], m("wout"), yo[:, :, :].rearrange("p b t -> p (b t)"), start=True,
                   stop=True).then_inc(s_out_mm, 1)

            def fold_bias():
                pe.wait_ge(s_bfold_sum, STAGES)
                pe.wait_ge(s_p_done, 1)
                for k in range(HT):
                    last = mm(psM[:, 0, k:k + 1], bx[0:1, k * P:(k + 1) * P], cst("ident")[0:1, 0:1], start=True, stop=True)
                last.then_inc(s_ub_mm, 1)

            def fold_down():
                pe.wait_ge(s_fold_sum, 2 * STAGES)
                pe.wait_ge(s_lgT_read, 2)
                for k in range(HT):
                    last = nc.tensor.transpose(psM[:, 1, k * P:(k + 1) * P], wc[:, k * P:(k + 1) * P], cst("ident"))
                last.then_inc(s_wcT_mm, 1)

            def ffn(v):
                pe.wait_ge(s_ln_h, ln_ffn(v) + 1)
                pe.wait_ge(s_zo_done, v + 1)
                pe.wait_ge(s_a_raw, v + 1)
                for k in range(HT):
                    if k >= 2:
                        pe.wait_ge(s_u_done, HT * v + k - 1)
                    mm(psF[k % 2][:, :], wx[:, k * P:(k + 1) * P], hS[:, :], start=True, stop=True).then_inc(s_u_mm, 1)
                if v == 0:
                    pe.wait_ge(s_wcT_done, 1)
                pe.wait_ge(s_acc0_done, min(v + 2, WINDOWS))
                if v > 0:
                    pe.wait_ge(s_ffn_read, v)
                for k in range(HT):
                    pe.wait_ge(s_u_done, HT * v + k + 1)
                    last = mm(psM[:, 0, :], wcT[:, k, :], u[:, k, :], start=(k == 0), stop=(k == HT - 1))
                last.then_inc(s_ffn_mm, 1)

            pe.wait_ge(s_const_in, 16)
            pe.wait_ge(s_x0_in, 16)
            ln(0, x[:, 0, :])
            modulation()
            pe.wait_ge(s_x_in, 16 * (WINDOWS - 1))
            for w in range(1, WINDOWS):
                ln(ln_front(w), x[:, w, :])
            pe.wait_ge(s_mat_in, 16)
            project(0)
            square_sums(0)
            key_products(0)
            fold_bias()
            for w in range(WINDOWS + 1):
                v, n = w - 1, w + 1
                if v >= 0:
                    experts_back(v)
                if w < WINDOWS:
                    if w == 0:
                        pe.wait_ge(s_exp_in, 16 * 5)
                    attn_out(w)
                if n < WINDOWS:
                    project(n)
                if v >= 0:
                    pe.wait_ge(s_x2_done, v + 1)
                    ln(ln_ssd(v), x[:, v, :])
                if w < WINDOWS:
                    pe.wait_ge(s_x1_done, w + 1)
                    ln(ln_moe(w), x[:, w, :])
                if v >= 0:
                    ssd_in(v)
                if w < WINDOWS:
                    router(w)
                if n < WINDOWS:
                    square_sums(n)
                if w < WINDOWS:
                    router_bias(w)
                if v >= 0:
                    ssd_out(v)
                if n < WINDOWS:
                    key_products(n)
                if v == 0:
                    fold_down()
                if v >= 0:
                    pe.wait_ge(s_x3_done, v + 1)
                    ln(ln_ffn(v), x[:, v, :])
                    ffn(v)
                if w < WINDOWS:
                    if w == 0:
                        pe.wait_ge(s_we1_in, 16)
                        pe.wait_ge(s_we2_in, 16)
                    experts(w)

        @block.scalar
        def _(act):
            def ln(n):
                act.wait_ge(s_ln_c, n + 1)
                nc.scalar.activation(sq[:, :], psA[:, :], ACT.Square).then_inc(s_ln_sq, 1)
                act.wait_ge(s_ln_v, n + 1)
                nc.scalar.activation(rs[:, :], psB[:, :], ACT.Ln, bias=eps[:, 0:1]).then_inc(s_ln_log, 1)
                act.wait_ge(s_ln_log, n + 1)
                nc.scalar.activation(rs[:, :], rs[:, :], ACT.Exp, scale=-0.5).then_inc(s_ln_sd, 1)

            def projected(n):
                act.wait_ge(s_carry_done, n + 1)
                cols = TW if n + 1 < WINDOWS else TW - 1
                if n == 0:
                    act.wait_ge(s_proj0_mm, 1)
                    b = psM[:, 0, 0:3 * NB].rearrange("p (i b) -> p i b", i=3)
                    for i, name in enumerate(["bq", "bk", "bv"]):
                        last = nc.scalar.activation(p[:, i, :, HALO - 1], b[:, i, :], ACT.Silu, bias=pc(name))
                    last.then_inc(s_p_done, 1)
                for i, (b, name) in enumerate(zip([psF[0], psF[1], psS[0]], ["bq", "bk", "bv"])):
                    act.wait_ge(s_proj_mm, 5 * n + i + 1)
                    nc.scalar.activation(p[:, i, :, HALO:HALO + cols], b[:, 0:NB * cols].rearrange("p (b t) -> p b t", b=NB),
                                         ACT.Silu, bias=pc(name)).then_inc(s_p_done, 1)
                act.wait_ge(s_proj_mm, 5 * n + 5)
                if n > 0:
                    act.wait_ge(s_xk_init, n)
                nc.scalar.activation(ag[:, :], psS[1][:, :], ACT.Sigmoid, bias=pc("ba")).then_inc(s_gates_done, 1)
                nc.scalar.activation(bg[:, :], psM[:, 1, :], ACT.Sigmoid, bias=pc("bb")).then_inc(s_gates_done, 1)

            def convolved(n):
                act.wait_ge(s_conv_tap, 3 * TAPS * (n + 1))
                nc.scalar.activation(c3[:, :, :], y[:, :, :], ACT.Silu).then_inc(s_c3_done, 1)
                act.wait_ge(s_c3_done, n + 1)
                if n > 0:
                    act.wait_ge(s_attn_mm, n)
                nc.scalar.activation(sq2[:, :, :], c3[:, 0:2, :], ACT.Square).then_inc(s_l2_sq, 1)

            def norms(n):
                act.wait_ge(s_l2_mm, 2 * (n + 1))
                for i in range(2):
                    nc.scalar.activation(nrm[:, i, :], psS[i][:, :], ACT.Sqrt, scale=float(P)).then_inc(s_l2_root, 1)
                act.wait_ge(s_l2_root, 2 * (n + 1))
                nc.scalar.activation(nrm[:, :, :], nrm[:, :, :], ACT.Ln, bias=eps[:, 1:2]).then_inc(s_l2_log, 1)
                act.wait_ge(s_l2_log, n + 1)
                nc.scalar.activation(nrm[:, :, :], nrm[:, :, :], ACT.Exp, scale=-1.0).then_inc(s_l2_rn, 1)

            def decays(w, c):
                g = NCH * w + c
                if g - 1 > 0:
                    act.wait_ge(s_scan_done, g - 1)
                a = bt(ag[:, :])[:, :, c * CH:(c + 1) * CH].unsqueeze(2).broadcast_to([P, NB, DH, CH])
                nc.scalar.activation(A9[g % 2][:, :, 1:CH + 1].rearrange("p (b e) i -> p b e i", b=NB), a,
                                     ACT.Copy).then_inc(s_a9_done, 1)

            def attn_branch(w):
                act.wait_ge(s_attn_mm, w + 1)
                if w > 0:
                    act.wait_ge(s_x1_done, w)
                nc.scalar.activation(br[:, :], psM[:, 0, :], ACT.Identity, bias=pc("bo")).then_inc(s_ao_done, 1)

            def router(w):
                act.wait_ge(s_r1_mm, w + 1)
                act.wait_ge(s_red_done, NCH * (w + 1))
                nc.scalar.activation(r1[:, :], psM[:, 1, :], ACT.Silu, bias=pc("rb1")).then_inc(s_r1_done, 1)
                act.wait_ge(s_ls_done, w + 1)
                nc.scalar.activation(ex[:, :, :], ls[:, :, :], ACT.Exp).then_inc(s_ex_done, 1)

            def router_bias(w):
                act.wait_ge(s_gT_mm, w + 1)
                nc.scalar.activation(gateT[:, :, :], psM[0:EXPERTS, 1, :].rearrange("e (t n) -> e t n", t=TT),
                                     ACT.Copy).then_inc(s_lgT_read, 1)
                act.wait_ge(s_acc0_mm, w + 1)
                if w > 0:
                    act.wait_ge(s_yT_mm, w)
                nc.scalar.activation(acc[:, :, :], psM[:, 0, :].rearrange("p (t n) -> p t n", t=TT), ACT.Copy).then_inc(s_acc0_done, 1)

            def experts(w):
                def hidden(e):
                    for k in range(HT):
                        n = HT * (EXPERTS * w + e) + k
                        act.wait_ge(s_hid_mm, n + 1)
                        if EXPERTS * w + e - 1 > 0:
                            act.wait_ge(s_eo_mm, EXPERTS * w + e - 1)
                        nc.scalar.activation(hid[(EXPERTS * w + e) % 2][:, k, :], psF[n % 2][:, :], ACT.Silu,
                                             bias=pc("be1", HT * e + k)).then_inc(s_hid_done, 1)

                def combine(e):
                    n = EXPERTS * w + e
                    act.wait_ge(s_eo_mm, n + 1)
                    if n - 1 > 0:
                        act.wait_ge(s_acc_done, n - 1)
                    for t in range(TT):
                        nc.scalar.activation(cmb[n % 2][:, t, :], psS[n % 2][:, t * P:(t + 1) * P], ACT.Copy,
                                             scale=gate[:, t, e:e + 1]).then_inc(s_cmb_done, 1)
                if w == 0:
                    act.wait_ge(s_fold_sum, 2 * STAGES)
                    act.wait_ge(s_ub_mm, 1)
                if w > 0:
                    act.wait_ge(s_ffn_mm, w)
                hidden(0)
                for e in range(1, EXPERTS):
                    hidden(e)
                    combine(e - 1)
                    if w + 1 < WINDOWS and e + 1 < NCH:
                        decays(w + 1, e + 1)
                combine(EXPERTS - 1)

            def ssd_in(v):
                act.wait_ge(s_in_mm, v + 1)
                act.wait_ge(s_halo_done, v + 1)
                nc.scalar.activation(xi[:, :, TAPS - 1:], bt(psF[0][:, :]), ACT.Copy).then_inc(s_xi_done, 1)
                act.wait_ge(s_dec_mm, v + 1)
                if v > 0:
                    act.wait_ge(s_nt_done, v)
                nc.scalar.activation(A[:, :], psF[1][:, :], ACT.Copy, scale=pc("wbase")).then_inc(s_a_raw, 1)

            def ssd_exp(v):
                act.wait_ge(s_dm_done, v + 1)
                nc.scalar.activation(EE[:, :, 1:], dm[:, :, 1:], ACT.Exp).then_inc(s_ee_done, 1)
                act.wait_ge(s_gd_done, v + 1)
                nc.scalar.activation(ge[:, :], gd[:, :], ACT.Exp).then_inc(s_ge_done, 1)
                act.wait_ge(s_so_done, v + 1)
                nc.scalar.activation(sde[:, :, :], so[:, :, :], ACT.Exp).then_inc(s_sde_done, 1)
                act.wait_ge(s_t8_done, v + 1)
                nc.scalar.activation(f8[:, :, :], t8[:, :, :], ACT.Exp).then_inc(s_f8_done, 1)
                act.wait_ge(s_nt_done, v + 1)
                nc.scalar.activation(no[:, :, :], no[:, :, :], ACT.Ln).then_inc(s_no_log, 1)
                act.wait_ge(s_no_log, v + 1)
                nc.scalar.activation(no[:, :, :], no[:, :, :], ACT.Exp, scale=-1.0).then_inc(s_rN_done, 1)

            def ffn(v):
                if v == 0:
                    act.wait_ge(s_wcT_mm, 1)
                    nc.scalar.activation(wcT[:, :, :], psM[:, 1, :].rearrange("p (t n) -> p t n", t=HT), ACT.Copy).then_inc(s_wcT_done, 1)
                    act.wait_ge(s_ub_done, 2)
                if v > 0:
                    act.wait_ge(s_ffn_mm, v)
                act.wait_ge(s_eo_mm, EXPERTS * (v + 1))
                for k in range(HT):
                    act.wait_ge(s_u_mm, HT * v + k + 1)
                    nc.scalar.activation(u[:, k, :], psF[k % 2][:, :], ACT.Gelu, bias=ubias[:, k:k + 1]).then_inc(s_u_done, 1)
                act.wait_ge(s_ffn_mm, v + 1)
                act.wait_ge(s_x3_done, v + 1)
                nc.scalar.activation(brS[:, :], psM[:, 0, :], ACT.Identity, bias=dbias[:, 0:1]).then_inc(s_ffn_read, 1)

            act.wait_ge(s_mod_in, 32)
            nc.scalar.activation(csil[:, :, :], csil[:, :, :], ACT.Silu).then_inc(s_csil_done, 1)
            act.wait_ge(s_eps_set, 2)
            for w in range(WINDOWS):
                ln(ln_front(w))
            act.wait_ge(s_col_in, 16)
            projected(0)
            convolved(0)
            norms(0)
            act.wait_ge(s_gates_done, 2)
            for c in range(NCH):
                decays(0, c)
            for w in range(WINDOWS + 1):
                v, n = w - 1, w + 1
                if w < WINDOWS:
                    attn_branch(w)
                if n < WINDOWS:
                    projected(n)
                if v >= 0:
                    ln(ln_ssd(v))
                if n < WINDOWS:
                    convolved(n)
                if w < WINDOWS:
                    ln(ln_moe(w))
                if v >= 0:
                    ssd_in(v)
                if w < WINDOWS:
                    router(w)
                if n < WINDOWS:
                    norms(n)
                if w < WINDOWS:
                    router_bias(w)
                if v >= 0:
                    ssd_exp(v)
                if n < WINDOWS:
                    act.wait_ge(s_gates_done, 2 * (n + 1))
                    decays(n, 0)
                    decays(n, 1)
                if v >= 0:
                    ln(ln_ffn(v))
                    ffn(v)
                if w < WINDOWS:
                    experts(w)

        @block.vector
        def _(dve):
            v_ = nc.vector

            def ln(n, out):
                dve.wait_ge(s_ln_sd, n + 1)
                v_.tensor_tensor(out, bt(psA[:, :]), bt(rs[:, :]), ALU.mult).then_inc(s_ln_n1, 1)

            def modulation():
                dve.wait_ge(s_mod_mm, 1)
                v_.tensor_copy(mod[:, :, :], psM[:, 0, 0:12 * NB].rearrange("p (i b) -> p i b", b=NB)).then_inc(s_mod_read, 1)
                dve.wait_ge(s_mod_read, 1)
                scale = mod[:, 1:12:3, :]
                gates = mod[:, 2:12:3, :]
                v_.tensor_scalar(scale, scale, 1.0, None, ALU.add).then_inc(s_mod_scale, 1)
                v_.tensor_scalar(gsg[:, :, :], gates, 0.0, 2.0, ALU.is_ge, ALU.mult).then_inc(s_mod_sign, 1)
                v_.tensor_scalar(gab[:, :, :], gates, -1.0, None, ALU.mult).then_inc(s_mod_neg, 1)
                dve.wait_ge(s_mod_neg, 1)
                v_.tensor_tensor(gab[:, :, :], gab[:, :, :], gates, ALU.max).then_inc(s_mod_abs, 1)
                dve.wait_ge(s_mod_sign, 1)
                v_.tensor_scalar(gsg[:, :, :], gsg[:, :, :], -1.0, None, ALU.add).then_inc(s_mod_sign, 1)
                dve.wait_ge(s_mod_abs, 1)
                v_.tensor_scalar(gab[:, :, :], gab[:, :, :], 0.25, None, ALU.max).then_inc(s_mod_abs, 1)
                dve.wait_ge(s_mod_sign, 2)
                dve.wait_ge(s_mod_abs, 2)
                v_.tensor_tensor(gates, gsg[:, :, :], gab[:, :, :], ALU.mult).then_inc(s_mod_done, 1)

            def bias_fold():
                dve.wait_ge(s_fold_in, 48)
                for s in range(STAGES):
                    dve.wait_ge(s_coef_in[s % 2], 16 * (s // 2 + 1))
                    if s > 0:
                        dve.wait_ge(s_bfold_sum, s)
                    pr = bx[:, :].rearrange("p (n h s) -> p n h s", h=2, s=1 << s)
                    d = fb[:, 1, :].rearrange("p (n h s) -> p n h s", h=2, s=1 << s)
                    o = coef[s % 2][0:1, 1, :].rearrange("p (n h s) -> p n h s", h=2, s=1 << s)
                    v_.tensor_tensor(fb[:, 0, :], bx[:, :], coef[s % 2][0:1, 0, :], ALU.mult).then_inc(s_bfold_diag, 1)
                    for h in range(2):
                        v_.tensor_tensor(d[:, :, h, :], pr[:, :, 1 - h, :], o[:, :, h, :], ALU.mult).then_inc(s_bfold_off, 1)
                    dve.wait_ge(s_bfold_off, 2 * (s + 1))
                    dve.wait_ge(s_bfold_diag, s + 1)
                    v_.tensor_tensor(bx[:, :], fb[:, 0, :], fb[:, 1, :], ALU.add).then_inc(s_bfold_sum, 1)

            def carry(w):
                if w > 0:
                    v_.tensor_copy(p[:, :, :, 0:HALO], p[:, :, :, TW:TW + HALO]).then_inc(s_carry_done, 1)
                    if w + 1 == WINDOWS:
                        dve.wait_ge(s_carry_done, w + 1)
                        v_.memset(p[:, :, :, TW + HALO - 1:], 0.0).then_inc(s_pad_set, 1)
                        dve.wait_ge(s_pad_set, 1)

            def convolve(w):
                dve.wait_ge(s_carry_done, w + 1)
                dve.wait_ge(s_p_done, 3 * (w + 1) + 1)
                for j in range(TAPS):
                    for i, name in enumerate(["cq", "ck", "cv"]):
                        src = p[:, i, :, j:j + TW]
                        if j == 0:
                            v_.tensor_scalar(bt(y[:, i, :]), src, pc(name, j), None, ALU.mult).then_inc(s_conv_tap, 1)
                        else:
                            dve.wait_ge(s_conv_tap, 3 * (TAPS * w + j - 1) + i + 1)
                            v_.scalar_tensor_tensor(bt(y[:, i, :]), src, pc(name, j), bt(y[:, i, :]), ALU.mult,
                                                   ALU.add).then_inc(s_conv_tap, 1)

            def couple(w):
                n = 0
                for g, js in enumerate(PACK):
                    dve.wait_ge(s_kk_mm, 4 * w + g + 1)
                    at = 0
                    for j in js:
                        n += 1
                        k = CH - 1 - j
                        dve.wait_ge(s_g_done, 7 * w + CH - 1 - j)
                        dve.wait_ge(s_cp_done, w + 1)
                        v_.tensor_tensor(Mj[j][:, :, :], psS[g % 2][:, at:at + BC * k].rearrange("p (g i) -> p g i", i=k),
                                        G[j][:, :, 1:], ALU.mult).then_inc(s_mj_done, 1)
                        at += BC * k

            def solve_keys(w):
                dve.wait_ge(s_xk_init, w + 1)
                dve.wait_ge(s_mj_done, 7 * (w + 1))
                X = bci(XK[:, :])
                for j in range(CH - 1):
                    k = CH - 1 - j
                    if 7 * w + j > 0:
                        dve.wait_ge(s_xk_sub, 7 * w + j)
                    tmp = tk[:, 0:BC * k].rearrange("p (g i) -> p g i", i=k)
                    v_.tensor_tensor(tmp, Mj[j][:, :, :], X[:, :, j:j + 1].broadcast_to([P, BC, k]), ALU.mult).then_inc(s_xk_prod, 1)
                    dve.wait_ge(s_xk_prod, 7 * w + j + 1)
                    v_.tensor_tensor(X[:, :, j + 1:], X[:, :, j + 1:], tmp, ALU.subtract).then_inc(s_xk_sub, 1)

            def scan(w):
                dve.wait_ge(s_krep_in, 16 * DH * (w + 1))
                dve.wait_ge(s_wrep_in, 16 * DH * (w + 1))
                dve.wait_ge(s_xv_sub, 7 * (w + 1))
                if w > 0:
                    dve.wait_ge(s_acc0_mm, w)
                for c in range(NCH):
                    g = NCH * w + c
                    t0, t1 = c * CH, (c + 1) * CH
                    prev = H[(g - 1) % NH_][:, :, CH].rearrange("p (b e) -> p b e", b=NB)
                    wv = wrep[:, :, :].rearrange("p e (b t) -> p b e t", b=NB)[:, :, :, t0:t1]
                    kv = krep[:, :, :].rearrange("p e (b t) -> p b e t", b=NB)[:, :, :, t0:t1]
                    if g > 0:
                        dve.wait_ge(s_scan_done, g)
                    v_.tensor_tensor(Pb[:, :, :, :], wv, prev.unsqueeze(3).broadcast_to([P, NB, DH, CH]), ALU.mult).then_inc(s_prod_done, 1)
                    v_.tensor_copy(D1[:, :, 0], H[(g - 1) % NH_][:, :, CH]).then_inc(s_seed_done, 1)
                    dve.wait_ge(s_prod_done, g + 1)
                    v_.tensor_reduce(R[:, :, :], Pb[:, :, :, :].rearrange("p b e i -> p b i e"), AX.X, ALU.add).then_inc(s_red_done, 1)
                    dve.wait_ge(s_red_done, g + 1)
                    v_.tensor_tensor(U[:, :, :], bt(XV[:, :])[:, :, t0:t1], R[:, :, :], ALU.subtract).then_inc(s_u_delta, 1)
                    dve.wait_ge(s_u_delta, g + 1)
                    v_.tensor_tensor(D1[:, :, 1:].rearrange("p (b e) i -> p b e i", b=NB), kv,
                                    U[:, :, :].unsqueeze(2).broadcast_to([P, NB, DH, CH]), ALU.mult).then_inc(s_outer_done, 1)
                    dve.wait_ge(s_outer_done, g + 1)
                    dve.wait_ge(s_seed_done, g + 1)
                    dve.wait_ge(s_a9_done, g + 1)
                    if g - NH_ + 1 > 0:
                        dve.wait_ge(s_qs_done, g - NH_ + 1)
                    v_.tensor_tensor_scan(H[g % NH_][:, :, :].rearrange("p s i -> p (s i)"),
                                         A9[g % 2][:, :, :].rearrange("p s i -> p (s i)"),
                                         D1[:, :, :].rearrange("p s i -> p (s i)"), 0.0, ALU.mult,
                                         ALU.add).then_inc(s_scan_done, 1)

            def route(w):
                dve.wait_ge(s_lg_mm, w + 1)
                if 2 * w > 0:
                    dve.wait_ge(s_route_q, 2 * w)
                v_.tensor_tensor(lg[:, :, :], psM[:, 0, 0:TT * EXPERTS].rearrange("p (t e) -> p t e", e=EXPERTS),
                                rb2s[:, :].unsqueeze(1).broadcast_to([P, TT, EXPERTS]), ALU.add).then_inc(s_lg_done, 1)
                dve.wait_ge(s_lg_done, w + 1)
                v_.tensor_reduce(lmax[:, :], lg[:, :, :], AX.X, ALU.max).then_inc(s_lmax_done, 1)
                dve.wait_ge(s_lmax_done, w + 1)
                v_.tensor_tensor(ls[:, :, :], lg[:, :, :], lmax[:, :].unsqueeze(2).broadcast_to([P, TT, EXPERTS]), ALU.subtract).then_inc(s_ls_done, 1)
                if EXPERTS * w > 0:
                    dve.wait_ge(s_acc_done, EXPERTS * w)
                for t in range(TT):
                    mine = lg[:, t, :].unsqueeze(2).broadcast_to([P, EXPERTS, EXPERTS])
                    other = lg[:, t, :].unsqueeze(1).broadcast_to([P, EXPERTS, EXPERTS])
                    v_.tensor_tensor(gt[:, t, :, :], other, mine, ALU.is_gt).then_inc(s_cmp_done, 1)
                    v_.tensor_tensor(eq[:, t, :, :], other, mine, ALU.is_equal).then_inc(s_cmp_done, 1)
                dve.wait_ge(s_cmp_done, 2 * TT * (w + 1))
                v_.tensor_tensor(eq[:, :, :, :].rearrange("p t a b -> p t (a b)"), eq[:, :, :, :].rearrange("p t a b -> p t (a b)"),
                                low[:, :, :].rearrange("p a b -> p (a b)").unsqueeze(1).broadcast_to([P, TT, EXPERTS * EXPERTS]),
                                ALU.mult).then_inc(s_route_q, 1)
                dve.wait_ge(s_route_q, 2 * w + 1)
                v_.tensor_tensor(gt[:, :, :, :], gt[:, :, :, :], eq[:, :, :, :], ALU.add).then_inc(s_route_q, 1)
                dve.wait_ge(s_route_q, 2 * w + 2)
                v_.tensor_reduce(rank[:, :, :], gt[:, :, :, :], AX.X, ALU.add).then_inc(s_rank_done, 1)
                dve.wait_ge(s_rank_done, w + 1)
                dve.wait_ge(s_ex_done, w + 1)
                v_.scalar_tensor_tensor(exm[:, :, :], rank[:, :, :], 1.5, ex[:, :, :], ALU.is_lt, ALU.mult).then_inc(s_exm_done, 1)
                dve.wait_ge(s_exm_done, w + 1)
                v_.tensor_reduce(den[:, :], exm[:, :, :], AX.X, ALU.add).then_inc(s_den_done, 1)
                dve.wait_ge(s_den_done, w + 1)
                v_.reciprocal(rden[:, :], den[:, :]).then_inc(s_rden_done, 1)
                dve.wait_ge(s_rden_done, w + 1)
                if TT * EXPERTS * w > 0:
                    dve.wait_ge(s_cmb_done, TT * EXPERTS * w)
                v_.tensor_tensor(gate[:, :, :], exm[:, :, :], rden[:, :].unsqueeze(2).broadcast_to([P, TT, EXPERTS]), ALU.mult).then_inc(s_gate_done, 1)

            def experts_branch(v):
                dve.wait_ge(s_yT_mm, v + 1)
                if v > 0:
                    dve.wait_ge(s_x4_done, v)
                v_.tensor_tensor(brS[:, :], psS[0][:, :], h2[:, :], ALU.add).then_inc(s_yf_done, 1)

            def ssd_halo(v):
                if v == 0:
                    v_.memset(xi[:, :, 0:HALO], 0.0).then_inc(s_halo_done, 1)
                else:
                    dve.wait_ge(s_xc_tap, 4 * v)
                    v_.tensor_copy(xi[:, :, 0:HALO], xi[:, :, TW:TW + HALO]).then_inc(s_halo_done, 1)

            def flat(ap):
                return ap.rearrange("p b t -> p (b t)")

            def ssd_decay(v):
                dve.wait_ge(s_a_raw, v + 1)
                v_.tensor_tensor_scan(flat(ac[:, :, :]), flat(segm[:, :, :]), A[:, :], 0.0, ALU.mult, ALU.add).then_inc(s_ac_done, 1)
                dve.wait_ge(s_halo_done, v + 1)
                dve.wait_ge(s_xi_done, v + 1)
                v_.tensor_scalar(bt(xc[:, :]), xi[:, :, 0:TW], pc("cx", 0), pc("cb"), ALU.mult, ALU.add).then_inc(s_xc_tap, 1)
                dve.wait_ge(s_ac_done, v + 1)
                if v > 0:
                    dve.wait_ge(s_out_mm, v)
                v_.tensor_tensor_scan(flat(rm[:, :, :]), flat(segb[:, :, :]), flat(ac[:, :, :]), 0.0, ALU.add, ALU.min).then_inc(s_rm_done, 1)
                dve.wait_ge(s_xc_tap, 4 * v + 1)
                v_.scalar_tensor_tensor(bt(xc[:, :]), xi[:, :, 1:1 + TW], pc("cx", 1), bt(xc[:, :]), ALU.mult, ALU.add).then_inc(s_xc_tap, 1)
                dve.wait_ge(s_rm_done, v + 1)
                v_.tensor_tensor(dm[:, :, 1:], rm[:, :, 1:], rm[:, :, 0:TW - 1], ALU.subtract).then_inc(s_dm_done, 1)
                v_.tensor_tensor(gd[:, :], flat(rm[:, :, :]), flat(ac[:, :, :]), ALU.subtract).then_inc(s_gd_done, 1)
                dve.wait_ge(s_xc_tap, 4 * v + 2)
                v_.scalar_tensor_tensor(bt(xc[:, :]), xi[:, :, 2:2 + TW], pc("cx", 2), bt(xc[:, :]), ALU.mult, ALU.add).then_inc(s_xc_tap, 1)
                v_.tensor_tensor(t8[:, 0, :], Ms[v % 2][:, :], ac[:, :, TW - 1], ALU.add).then_inc(s_t8_a, 1)
                v_.tensor_reduce(mx[:, :], ac[:, :, :], AX.X, ALU.max).then_inc(s_mx_done, 1)
                dve.wait_ge(s_xc_tap, 4 * v + 3)
                v_.scalar_tensor_tensor(bt(xc[:, :]), xi[:, :, 3:3 + TW], pc("cx", 3), bt(xc[:, :]), ALU.mult, ALU.add).then_inc(s_xc_tap, 1)
                dve.wait_ge(s_mx_done, v + 1)
                v_.tensor_tensor(so[:, :, :], ac[:, :, :], mx[:, :].unsqueeze(2).broadcast_to([P, NB, TW]), ALU.subtract).then_inc(s_so_done, 1)
                dve.wait_ge(s_t8_a, v + 1)
                v_.tensor_scalar(Ms[(v + 1) % 2][:, :], t8[:, 0, :], 0.0, None, ALU.max).then_inc(s_ms_done, 1)
                dve.wait_ge(s_ms_done, v + 1)
                v_.tensor_scalar(t8[:, 1, :], Ms[(v + 1) % 2][:, :], -1.0, None, ALU.mult).then_inc(s_t8_n, 1)
                dve.wait_ge(s_t8_n, v + 1)
                v_.tensor_tensor(t8[:, 0, :], t8[:, 0, :], t8[:, 1, :], ALU.add).then_inc(s_t8_done, 1)

            def ssd_mix(v):
                dve.wait_ge(s_ge_done, v + 1)
                dve.wait_ge(s_xc_tap, 4 * v + 4)
                v_.tensor_tensor(gx[:, :], ge[:, :], xc[:, :], ALU.mult).then_inc(s_gx_done, 1)
                dve.wait_ge(s_ee_done, v + 1)
                dve.wait_ge(s_gx_done, v + 1)
                v_.tensor_tensor_scan(flat(N[:, :, :]), flat(EE[:, :, :]), ge[:, :], 0.0, ALU.mult, ALU.add).then_inc(s_nd_done, 1)
                v_.tensor_tensor_scan(flat(Y[:, :, :]), flat(EE[:, :, :]), gx[:, :], 0.0, ALU.mult, ALU.add).then_inc(s_n_done, 1)
                dve.wait_ge(s_sde_done, v + 1)
                if v > 0:
                    dve.wait_ge(s_hs_done, v)
                v_.tensor_tensor(yo[:, :, :], sde[:, :, :], Hs[:, 0, :].unsqueeze(2).broadcast_to([P, NB, TW]), ALU.mult).then_inc(s_no_done, 1)
                v_.tensor_tensor(no[:, :, :], sde[:, :, :], Hs[:, 1, :].unsqueeze(2).broadcast_to([P, NB, TW]), ALU.mult).then_inc(s_no_done, 1)
                dve.wait_ge(s_nd_done, v + 1)
                dve.wait_ge(s_no_done, 2 * v + 2)
                v_.tensor_tensor(no[:, :, :], no[:, :, :], N[:, :, :], ALU.add).then_inc(s_nt_done, 1)
                dve.wait_ge(s_n_done, v + 1)
                v_.tensor_tensor(yo[:, :, :], yo[:, :, :], Y[:, :, :], ALU.add).then_inc(s_yt_done, 1)
                dve.wait_ge(s_f8_done, v + 1)
                v_.tensor_tensor(Hs[:, :, :], Hs[:, :, :], f8[:, 0:1, :].broadcast_to([P, 2, NB]), ALU.mult).then_inc(s_hs_a, 1)
                v_.tensor_tensor(Yl[:, 0, :], Y[:, :, TW - 1], f8[:, 1, :], ALU.mult).then_inc(s_hs_a, 1)
                v_.tensor_tensor(Yl[:, 1, :], N[:, :, TW - 1], f8[:, 1, :], ALU.mult).then_inc(s_hs_a, 1)
                dve.wait_ge(s_hs_a, 3 * (v + 1))
                v_.tensor_tensor(Hs[:, :, :], Hs[:, :, :], Yl[:, :, :], ALU.add).then_inc(s_hs_done, 1)
                dve.wait_ge(s_rN_done, v + 1)
                dve.wait_ge(s_yt_done, v + 1)
                v_.tensor_tensor(yo[:, :, :], yo[:, :, :], no[:, :, :], ALU.mult).then_inc(s_yn_done, 1)

            def ssd_branch(v):
                dve.wait_ge(s_out_mm, v + 1)
                v_.tensor_tensor(bt(brS[:, :]), bt(psF[0][:, :]), per_b(GA, 1), ALU.mult).then_inc(s_zo_done, 1)

            v_.memset(eps[:, 0:1], 1.0e-5).then_inc(s_eps_set, 1)
            v_.memset(eps[:, 1:2], 1.0e-6).then_inc(s_eps_set, 1)
            v_.memset(p[:, :, :, 0:HALO - 1], 0.0).then_inc(s_carry_done, 1)
            for i in range(2):
                v_.memset(A9[i][:, :, 0], 0.0).then_inc(s_set, 1)
            v_.memset(H[NH_ - 1][:, :, CH], 0.0).then_inc(s_set, 1)
            v_.memset(segm[:, :, :], 1.0).then_inc(s_set, 1)
            v_.memset(segb[:, :, :], 0.0).then_inc(s_set, 1)
            v_.memset(EE[:, :, 0], 0.0).then_inc(s_set, 1)
            v_.memset(Ms[0][:, :], 0.0).then_inc(s_set, 1)
            v_.memset(Hs[:, :, :], 0.0).then_inc(s_set, 1)
            dve.wait_ge(s_set, 8)
            v_.memset(segm[:, :, 0], 0.0).then_inc(s_set, 1)
            v_.memset(segb[:, :, 0], BIG).then_inc(s_set, 1)
            dve.wait_ge(s_set, 10)
            ln(0, hf[:, :, 0:TW])
            modulation()
            for w in range(1, WINDOWS):
                ln(ln_front(w), hf[:, :, w * TW:(w + 1) * TW])
            dve.wait_ge(s_col_in, 16)
            v_.tensor_tensor(dbias[:, :], pc("bcon"), pc("downb"), ALU.add).then_inc(s_ub_done, 1)
            carry(0)
            convolve(0)
            couple(0)
            solve_keys(0)
            bias_fold()
            dve.wait_ge(s_ub_mm, 1)
            v_.tensor_tensor(ubias[:, :], psM[:, 0, 0:HT], col[:, COL["upb"]:COL["upb"] + HT], ALU.add).then_inc(s_ub_done, 1)
            scan(0)
            for w in range(WINDOWS + 1):
                v, n = w - 1, w + 1
                if v >= 0:
                    experts_branch(v)
                if n < WINDOWS:
                    carry(n)
                if v >= 0:
                    ssd_halo(v)
                    if HT * v > 0:
                        dve.wait_ge(s_u_mm, HT * v)
                    ln(ln_ssd(v), bt(hS[:, :]))
                if n < WINDOWS:
                    convolve(n)
                if w < WINDOWS:
                    if HT * EXPERTS * w > 0:
                        dve.wait_ge(s_hid_mm, HT * EXPERTS * w)
                    ln(ln_moe(w), bt(h2[:, :]))
                if v >= 0:
                    ssd_decay(v)
                if w < WINDOWS:
                    if w == 0:
                        dve.wait_ge(s_exp_in, 16 * 5)
                    route(w)
                if v >= 0:
                    ssd_mix(v)
                if n < WINDOWS:
                    couple(n)
                if v >= 0:
                    ssd_branch(v)
                    ln(ln_ffn(v), bt(hS[:, :]))
                if n < WINDOWS:
                    solve_keys(n)
                    scan(n)

        @block.gpsimd
        def _(pool):
            g_ = nc.gpsimd

            def ln(n, out, s, c, l):
                pool.wait_ge(s_ln_n1, n + 1)
                g_.tensor_tensor(out, out, per_b(c, l), ALU.mult).then_inc(s_ln_n2, 1)
                pool.wait_ge(s_ln_n2, n + 1)
                g_.tensor_tensor(out, out, per_b(s, l), ALU.add).then_inc(s_ln_h, 1)

            def decay_products(w):
                a = bci(ag[:, :])
                if 7 * w > 0:
                    pool.wait_ge(s_xk_prod, 7 * w)
                pool.wait_ge(s_gates_done, 2 * (w + 1))
                for j in reversed(range(CH - 1)):
                    n = 7 * w + CH - 2 - j
                    if n > 0:
                        pool.wait_ge(s_g_done, n)
                    g_.tensor_tensor(G[j][:, :, 1:], G[j + 1][:, :, :], a[:, :, j + 1:j + 2].broadcast_to([P, BC, CH - 1 - j]),
                                     ALU.mult).then_inc(s_g_done, 1)
                pool.wait_ge(s_g_done, 7 * (w + 1))
                if 16 * w > 0:
                    pool.wait_ge(s_xk_out, 16 * w)
                g_.tensor_tensor(bci(cpd[:, :]), G[0][:, :, :], a[:, :, 0:1].broadcast_to([P, BC, CH]), ALU.mult).then_inc(s_cp_done, 1)

            def keys(w):
                pool.wait_ge(s_l2_rn, w + 1)
                g_.tensor_tensor(kn[:, :], c3[:, 1, :], nrm[:, 1, :], ALU.mult).then_inc(s_kn_done, 1)
                g_.tensor_tensor(qn[:, :], c3[:, 0, :], nrm[:, 0, :], ALU.mult).then_inc(s_qn_done, 1)
                pool.wait_ge(s_kn_done, w + 1)
                g_.tensor_tensor(kb[:, :], kn[:, :], bg[:, :], ALU.mult).then_inc(s_kb_done, 1)
                pool.wait_ge(s_kb_done, w + 1)
                pool.wait_ge(s_qn_done, w + 1)
                k3, b3 = bci(kn[:, :]), bci(kb[:, :])
                for g, js in enumerate(PACK):
                    at = 0
                    for j in js:
                        k = CH - 1 - j
                        g_.tensor_tensor(KK[:, g, at:at + BC * k].rearrange("p (g i) -> p g i", i=k), b3[:, :, j + 1:],
                                         k3[:, :, j:j + 1].broadcast_to([P, BC, k]), ALU.mult).then_inc(s_kk_done, 1)
                        at += BC * k
                pool.wait_ge(s_cp_done, w + 1)
                g_.tensor_tensor(XK[:, :], kb[:, :], cpd[:, :], ALU.mult).then_inc(s_xk_init, 1)
                g_.tensor_tensor(XV[:, :], c3[:, 2, :], bg[:, :], ALU.mult).then_inc(s_vb_done0, 1)

            def solve_values(w):
                pool.wait_ge(s_mj_done, 7 * (w + 1))
                pool.wait_ge(s_vb_done0, w + 1)
                X = bci(XV[:, :])
                for j in range(CH - 1):
                    k = CH - 1 - j
                    if 7 * w + j > 0:
                        pool.wait_ge(s_xv_sub, 7 * w + j)
                    tmp = tv[:, 0:BC * k].rearrange("p (g i) -> p g i", i=k)
                    g_.tensor_tensor(tmp, Mj[j][:, :, :], X[:, :, j:j + 1].broadcast_to([P, BC, k]), ALU.mult).then_inc(s_xv_prod, 1)
                    pool.wait_ge(s_xv_prod, 7 * w + j + 1)
                    g_.tensor_tensor(X[:, :, j + 1:], X[:, :, j + 1:], tmp, ALU.subtract).then_inc(s_xv_sub, 1)

            def read_state(w, c):
                g = NCH * w + c
                pool.wait_ge(s_scan_done, g + 1)
                pool.wait_ge(s_qn_done, w + 1)
                q = bt(qn[:, :])[:, :, c * CH:(c + 1) * CH].unsqueeze(2).broadcast_to([P, NB, DH, CH])
                o = QS[:, :, :].rearrange("p e (b t) -> p b e t", b=NB)[:, :, :, c * CH:(c + 1) * CH]
                g_.tensor_tensor(o, H[g % NH_][:, :, 1:].rearrange("p (b e) i -> p b e i", b=NB), q, ALU.mult).then_inc(s_qs_done, 1)

            def fold(s):
                w_ = wx if s < STAGES else wc
                st = s if s < STAGES else 2 * STAGES - 1 - s
                pool.wait_ge(s_fold_in, 48)
                pool.wait_ge(s_coef_in[s % 2], 16 * (s // 2 + 1))
                if s > 0:
                    pool.wait_ge(s_fold_sum, s)
                v4 = w_[:, :].rearrange("p (n h s) -> p n h s", h=2, s=1 << st)
                d4 = ft[:, 1, :].rearrange("p (n h s) -> p n h s", h=2, s=1 << st)
                o4 = coef[s % 2][:, 1, :].rearrange("p (n h s) -> p n h s", h=2, s=1 << st)
                g_.tensor_tensor(ft[:, 0, :], w_[:, :], coef[s % 2][:, 0, :], ALU.mult).then_inc(s_fold_diag, 1)
                for h in range(2):
                    g_.tensor_tensor(d4[:, :, h, :], v4[:, :, 1 - h, :], o4[:, :, h, :], ALU.mult).then_inc(s_fold_off, 1)
                pool.wait_ge(s_fold_diag, s + 1)
                pool.wait_ge(s_fold_off, 2 * (s + 1))
                g_.tensor_tensor(w_[:, :], ft[:, 0, :], ft[:, 1, :], ALU.add).then_inc(s_fold_sum, 1)

            def add_expert(w, e):
                n = EXPERTS * w + e
                pool.wait_ge(s_cmb_done, TT * (n + 1))
                pool.wait_ge(s_acc0_done, w + 1)
                if n > 0:
                    pool.wait_ge(s_acc_done, n)
                g_.tensor_tensor(acc[:, :, :], acc[:, :, :], cmb[n % 2][:, :, :], ALU.add).then_inc(s_acc_done, 1)

            for j in range(CH):
                g_.memset(G[j][:, :, 0], 1.0).then_inc(s_g_set, 1)
            pool.wait_ge(s_g_set, CH)
            pool.wait_ge(s_mod_done, 1)
            pool.wait_ge(s_mod_scale, 1)
            for w in range(WINDOWS):
                ln(ln_front(w), hf[:, :, w * TW:(w + 1) * TW], SA, CA, 0)
            decay_products(0)
            keys(0)
            solve_values(0)
            for s in range(STAGES):
                fold(s)
            for c in range(NCH):
                fold(STAGES + c)
                read_state(0, c)
            fold(2 * STAGES - 1)
            for w in range(WINDOWS + 1):
                v, n = w - 1, w + 1
                if v >= 0:
                    pool.wait_ge(s_yf_done, v + 1)
                    g_.tensor_tensor(bt(brS[:, :]), bt(brS[:, :]), per_b(GB, 0), ALU.mult).then_inc(s_yg_done, 1)
                    pool.wait_ge(s_yg_done, v + 1)
                    g_.tensor_tensor(x[:, v, :], x[:, v, :], brS[:, :], ALU.add).then_inc(s_x2_done, 1)
                if w < WINDOWS:
                    pool.wait_ge(s_ao_done, w + 1)
                    g_.tensor_tensor(bt(br[:, :]), bt(br[:, :]), per_b(GA, 0), ALU.mult).then_inc(s_aog_done, 1)
                    pool.wait_ge(s_aog_done, w + 1)
                    g_.tensor_tensor(x[:, w, :], x[:, w, :], br[:, :], ALU.add).then_inc(s_x1_done, 1)
                if v >= 0:
                    ln(ln_ssd(v), bt(hS[:, :]), SA, CA, 1)
                if n < WINDOWS:
                    decay_products(n)
                if w < WINDOWS:
                    ln(ln_moe(w), bt(h2[:, :]), SB, CB, 0)
                if n < WINDOWS:
                    keys(n)
                if v >= 0:
                    pool.wait_ge(s_zo_done, v + 1)
                    g_.tensor_tensor(x[:, v, :], x[:, v, :], brS[:, :], ALU.add).then_inc(s_x3_done, 1)
                    ln(ln_ffn(v), bt(hS[:, :]), SB, CB, 1)
                if n < WINDOWS:
                    solve_values(n)
                if v >= 0:
                    pool.wait_ge(s_ffn_read, v + 1)
                    g_.tensor_tensor(bt(brS[:, :]), bt(brS[:, :]), per_b(GB, 1), ALU.mult).then_inc(s_y4_done, 1)
                    pool.wait_ge(s_y4_done, v + 1)
                    g_.tensor_tensor(x[:, v, :], x[:, v, :], brS[:, :], ALU.add).then_inc(s_x4_done, 1)
                if w < WINDOWS:
                    for e in range(EXPERTS):
                        add_expert(w, e)
                        if n < WINDOWS:
                            read_state(n, e)


def kernel(**inputs):
    import concourse.bacc as bacc
    from concourse.bass_utils import run_bass_kernel_spmd as run

    a = {k: np.asarray(v) for k, v in inputs.items()}
    f32 = np.float32

    xT = a["L0_attn_x"].reshape(NB, WINDOWS, TW, P).transpose(3, 1, 0, 2).reshape(P, WINDOWS, COLS)
    rep = lambda v, axis=0: np.repeat(v, DH, axis=axis)
    win = a["L1_attn_in_proj_w"]
    mats = np.stack([a["L0_attn_Wq"].T, a["L0_attn_Wk"].T, a["L0_attn_Wv"].T, rep(a["L0_attn_Wa"]).T,
                     rep(a["L0_attn_Wb"]).T, a["L0_ffn_rw1"], win[:P].T, rep(win[P:]).T, a["L1_attn_out_proj_w"].T], axis=1)
    head = np.arange(P) // DH
    eye = np.eye(P, dtype=f32)
    consts = np.stack([eye - f32(1.0 / P), np.full((P, P), 1.0 / P, f32),
                       (head[:, None] == head[None, :]).astype(f32), eye], axis=1)
    cols = np.concatenate([
        a["L0_attn_bq"][:, None], a["L0_attn_bk"][:, None], a["L0_attn_bv"][:, None],
        rep(a["L0_attn_ba"])[:, None], rep(a["L0_attn_bb"])[:, None], a["L0_attn_bo"][:, None], a["L0_ffn_rb1"][:, None],
        a["L0_attn_conv_q"][:, 0], a["L0_attn_conv_k"][:, 0], a["L0_attn_conv_v"][:, 0], a["L1_attn_conv_w"][:, 0],
        a["L1_attn_conv_b"][:, None], rep(a["L1_attn_w_base"])[:, None],
        a["L0_ffn_be1"].reshape(EXPERTS * HT, P).T, a["L1_ffn_up_bias"].reshape(HT, P).T,
        a["L1_ffn_b_con"][:, None], a["L1_ffn_down_bias"][:, None]], axis=1)
    cT = np.stack([a["L0_c"].T, a["L1_c"].T], axis=1)
    wmod = np.stack([a["L0_wmod"], a["L1_wmod"]], axis=1)
    wo_rep = rep(a["L0_attn_Wo"].T.reshape(HEADS, DH, P))
    we1 = a["L0_ffn_we1"].transpose(1, 0, 2)
    we2 = a["L0_ffn_we2"].reshape(EXPERTS, HT, P, P).transpose(2, 0, 1, 3)
    lower = np.tril(np.ones((EXPERTS, EXPERTS), f32), -1)

    def coefficients(wts, transposed):
        out = []
        order = range(STAGES)
        for s in (reversed(order) if transposed else order):
            q = wts[s].reshape(-1, 1 << s, 2, 2)
            same = np.stack([q[:, :, 0, 0], q[:, :, 1, 1]], axis=1)
            cross = [q[:, :, 0, 1], q[:, :, 1, 0]]
            cross = np.stack(cross[::-1] if transposed else cross, axis=1)
            out.append(np.stack([same.reshape(-1), cross.reshape(-1)]))
        return np.stack(out)

    arrays = {
        "xT": xT, "mats": mats, "consts": consts, "cols": cols, "cT": cT, "wmod": wmod, "wo_rep": wo_rep,
        "rw2": a["L0_ffn_rw2"], "rb2": a["L0_ffn_rb2"], "be2": a["L0_ffn_be2"], "we1": we1, "we2": we2,
        "lower": lower, "w_exp": a["L1_ffn_W_exp"], "b_exp": a["L1_ffn_b_exp"][None, :], "w_conT": a["L1_ffn_W_con"].T,
        "up_coef": coefficients(a["L1_ffn_up_weights"], False), "down_coef": coefficients(a["L1_ffn_down_weights"], True),
    }
    nc = bacc.Bacc("TRN2", target_bir_lowering=False, num_devices=1)
    feed, aps = {}, []
    for name, v in arrays.items():
        v = np.ascontiguousarray(v)
        feed[name + "_dram"] = v
        aps.append(nc.dram_tensor(name + "_dram", v.shape, mybir.dt.from_np(v.dtype), kind="ExternalInput").ap())
    aps.append(nc.dram_tensor("scratch_dram", [WINDOWS, 2, P, COLS], fp32, kind="Internal").ap())
    aps.append(nc.dram_tensor("outT_dram", [P, WINDOWS, COLS], fp32, kind="ExternalOutput").ap())
    program(nc, *aps)
    r = run(nc, [feed], core_ids=[0])
    got = r.results[0]["outT_dram"].reshape(P, WINDOWS, NB, TW)
    return np.ascontiguousarray(got.transpose(2, 1, 3, 0).reshape(NB, SEQ, P))
```
